# Optimizing a Trainium2 kernel written in Bass

```python
import numpy as np
import jax
import jax.numpy as jnp

def _softmax(x, axis=-1):
    return jax.nn.softmax(x, axis=axis)
def _gelu(x):
    return jax.nn.gelu(x, approximate=True)
def _silu(x):
    return jax.nn.silu(x)
def _sigmoid(x):
    return jax.nn.sigmoid(x)
def _layernorm(x, axis=-1, eps=1e-5):
    m = jnp.mean(x, axis=axis, keepdims=True)
    v = jnp.var(x, axis=axis, keepdims=True)
    return (x - m) / jnp.sqrt(v + eps)
def _scatter_add(tgt, idx, src, axis=0):
    return tgt.at[idx].add(src)
def _segment_sum(src, seg, n):
    return jax.ops.segment_sum(src, seg, n)

kernel_name = 'mk_conv_preact_d2_conv_nhwc256_f8c1e7'

def setup_inputs(seed: int = 0):
    np.random.seed(seed)
    _w = jnp.asarray
    def _rec_inputs():
        import jax
        import jax.numpy as jnp
        _gk = jax.random.key(seed)
        x = 7.22e-05 + 1 * jax.random.normal(jax.random.fold_in(_gk, 1), (1, 128, 256, 256), jnp.float32)
        return x
    x = _rec_inputs()
    def _L0_conv_setup():
        import jax, jax.numpy as jnp
        import numpy as np
        C_Z, H_Z, W_Z, NH, C = (128, 256, 256, 4, 64)
        EPS = 1e-05
        key = jax.random.key(seed)
        ks = jax.random.split(key, 8)
        s = 0.02
        return {'pair_rep': jax.random.normal(ks[0], (1, C_Z, H_Z, W_Z), jnp.float32), 'ln_w': jnp.ones((C_Z, H_Z, W_Z), jnp.float32), 'ln_b': jnp.zeros((C_Z, H_Z, W_Z), jnp.float32), 'wq': jax.random.normal(ks[1], (NH * C, C_Z), jnp.float32) * s, 'wk': jax.random.normal(ks[2], (NH * C, C_Z), jnp.float32) * s, 'wv': jax.random.normal(ks[3], (NH * C, C_Z), jnp.float32) * s, 'wb': jax.random.normal(ks[4], (NH, C_Z), jnp.float32) * s, 'wg_w': jax.random.normal(ks[5], (NH * C, C_Z), jnp.float32) * s, 'wg_b': jnp.zeros((NH * C,), jnp.float32), 'wrep_w': jax.random.normal(ks[6], (C_Z, NH * C), jnp.float32) * s, 'wrep_b': jnp.zeros((C_Z,), jnp.float32)}
    _L0_conv_all = _L0_conv_setup()
    _L0_conv_in = {k: v for k, v in _L0_conv_all.items() if k in ('ln_w', 'ln_b', 'wq', 'wk', 'wv', 'wb', 'wg_w', 'wg_b', 'wrep_w', 'wrep_b', )}
    del _L0_conv_all

    def _L1_conv_setup():
        import jax, jax.numpy as jnp
        import numpy as np
        QKV_DIM = 256
        C = 32
        N_HEAD = 8
        OUT_DIM = 256
        key = jax.random.key(seed)
        ks = jax.random.split(key, 9)
        hc = N_HEAD * C
        in_data = jax.random.normal(ks[0], (1, 128, 256, QKV_DIM), dtype=jnp.float32)
        nonbatched_bias = jax.random.normal(ks[1], (1, N_HEAD, 256, 256), dtype=jnp.float32)
        s = 1.0 / np.sqrt(QKV_DIM)
        Wq = jax.random.normal(ks[2], (hc, QKV_DIM), dtype=jnp.float32) * s
        Wk = jax.random.normal(ks[3], (hc, QKV_DIM), dtype=jnp.float32) * s
        Wv = jax.random.normal(ks[4], (hc, QKV_DIM), dtype=jnp.float32) * s
        Wg = jax.random.normal(ks[5], (hc, QKV_DIM), dtype=jnp.float32) * 0.02
        gating_bias = jnp.ones((hc,), dtype=jnp.float32)
        Wo = jax.random.normal(ks[6], (OUT_DIM, hc), dtype=jnp.float32) * 0.02
        bo = jnp.zeros((OUT_DIM,), dtype=jnp.float32)
        return {'in_data': in_data, 'nonbatched_bias': nonbatched_bias, 'Wq': Wq, 'Wk': Wk, 'Wv': Wv, 'Wg': Wg, 'gating_bias': gating_bias, 'Wo': Wo, 'bo': bo}
    _L1_conv_all = _L1_conv_setup()
    _L1_conv_in = {k: v for k, v in _L1_conv_all.items() if k in ('nonbatched_bias', 'Wq', 'Wk', 'Wv', 'Wg', 'gating_bias', 'Wo', 'bo', )}
    del _L1_conv_all

    return {
        "x": x,
        "L0_conv_ln_w": _L0_conv_in["ln_w"],
        "L0_conv_ln_b": _L0_conv_in["ln_b"],
        "L0_conv_wq": _L0_conv_in["wq"],
        "L0_conv_wk": _L0_conv_in["wk"],
        "L0_conv_wv": _L0_conv_in["wv"],
        "L0_conv_wb": _L0_conv_in["wb"],
        "L0_conv_wg_w": _L0_conv_in["wg_w"],
        "L0_conv_wg_b": _L0_conv_in["wg_b"],
        "L0_conv_wrep_w": _L0_conv_in["wrep_w"],
        "L0_conv_wrep_b": _L0_conv_in["wrep_b"],
        "L1_conv_nonbatched_bias": _L1_conv_in["nonbatched_bias"],
        "L1_conv_Wq": _L1_conv_in["Wq"],
        "L1_conv_Wk": _L1_conv_in["Wk"],
        "L1_conv_Wv": _L1_conv_in["Wv"],
        "L1_conv_Wg": _L1_conv_in["Wg"],
        "L1_conv_gating_bias": _L1_conv_in["gating_bias"],
        "L1_conv_Wo": _L1_conv_in["Wo"],
        "L1_conv_bo": _L1_conv_in["bo"],
    }

def reference(x, L0_conv_ln_w, L0_conv_ln_b, L0_conv_wq, L0_conv_wk, L0_conv_wv, L0_conv_wb, L0_conv_wg_w, L0_conv_wg_b, L0_conv_wrep_w, L0_conv_wrep_b, L1_conv_nonbatched_bias, L1_conv_Wq, L1_conv_Wk, L1_conv_Wv, L1_conv_Wg, L1_conv_gating_bias, L1_conv_Wo, L1_conv_bo):
    import jax
    import jax.numpy as jnp
    def _L0_conv_ref(pair_rep, ln_w, ln_b, wq, wk, wv, wb, wg_w, wg_b, wrep_w, wrep_b):
        import jax, jax.numpy as jnp
        import numpy as np
        C_Z, H_Z, W_Z, NH, C = (128, 256, 256, 4, 64)
        EPS = 1e-05
        B = pair_rep.shape[0]
        mu = jnp.mean(pair_rep, axis=(1, 2, 3), keepdims=True)
        var = jnp.var(pair_rep, axis=(1, 2, 3), keepdims=True)
        x = (pair_rep - mu) * jax.lax.rsqrt(var + EPS) * ln_w + ln_b

        def proj(w):
            y = jnp.einsum('oc,bcij->boij', w, x)
            return y.reshape(B, NH, C, H_Z, W_Z)
        q = proj(wq)
        k = proj(wk)
        v = proj(wv)
        g = jax.nn.sigmoid(proj(wg_w) + wg_b.reshape(1, NH, C, 1, 1))
        bias = jnp.einsum('hc,bcij->bhij', wb, x)
        scale = 1.0 / jnp.sqrt(jnp.float32(C))
        scores = jnp.einsum('bhcij,bhcik->bhijk', q, k) * scale + bias[:, :, None, :, :]
        a = jax.nn.softmax(scores, axis=-1)
        o = g * jnp.einsum('bhijk,bhcik->bhcij', a, v)
        o = o.transpose(0, 2, 1, 3, 4).reshape(B, C * NH, H_Z, W_Z)
        return jnp.einsum('oc,bcij->boij', wrep_w, o) + wrep_b.reshape(1, C_Z, 1, 1)

    def _L1_conv_ref(in_data, nonbatched_bias, Wq, Wk, Wv, Wg, gating_bias, Wo, bo):
        import jax, jax.numpy as jnp
        import numpy as np
        QKV_DIM = 256
        C = 32
        N_HEAD = 8
        OUT_DIM = 256
        scaling = C ** (-0.5)

        def proj(W):
            y = jnp.einsum('abld,ed->able', in_data, W)
            b1, b2, L, _ = y.shape
            return y.reshape(b1, b2, L, N_HEAD, C).transpose(0, 1, 3, 2, 4)
        q = proj(Wq) * scaling
        k = proj(Wk)
        v = proj(Wv)
        logits = jnp.einsum('abhqc,abhkc->abhqk', q, k)
        logits = logits + nonbatched_bias[:, None]
        weights = jax.nn.softmax(logits, axis=-1)
        wavg = jnp.einsum('abhqk,abhkc->abhqc', weights, v)
        b1, b2, H, L, c = wavg.shape
        wavg = wavg.transpose(0, 1, 3, 2, 4).reshape(b1, b2, L, H * c)
        gate = jax.nn.sigmoid(jnp.einsum('abld,ed->able', in_data, Wg) + gating_bias)
        wavg = gate * wavg
        out = jnp.einsum('able,oe->ablo', wavg, Wo) + bo
        return out

    def _gn(v, G=32, eps=1e-5):
        B_, H_, W_, C_ = v.shape
        g = v.reshape(B_, H_, W_, G, C_ // G)
        m = jnp.mean(g, axis=(1, 2, 4), keepdims=True)
        s = jnp.var(g, axis=(1, 2, 4), keepdims=True)
        return ((g - m) / jnp.sqrt(s + eps)).reshape(v.shape)

    def _ln_c(v, eps=1e-6):
        m = jnp.mean(v, axis=-1, keepdims=True)
        s = jnp.var(v, axis=-1, keepdims=True)
        return (v - m) / jnp.sqrt(s + eps)

    def _ln_t(v, eps=1e-5):
        m = jnp.mean(v, axis=-1, keepdims=True)
        s = jnp.var(v, axis=-1, keepdims=True)
        return (v - m) / jnp.sqrt(s + eps)

    def _to_tokens(v):
        B_, H_, W_, C_ = v.shape
        return v.reshape(B_, H_ * W_, C_)
    def _from_tokens(t, like):
        return t.reshape(like.shape)

    x = x + _L0_conv_ref(_gn(x), L0_conv_ln_w, L0_conv_ln_b, L0_conv_wq, L0_conv_wk, L0_conv_wv, L0_conv_wb, L0_conv_wg_w, L0_conv_wg_b, L0_conv_wrep_w, L0_conv_wrep_b)
    x = x + _L1_conv_ref(_gn(x), L1_conv_nonbatched_bias, L1_conv_Wq, L1_conv_Wk, L1_conv_Wv, L1_conv_Wg, L1_conv_gating_bias, L1_conv_Wo, L1_conv_bo)
    return x


_drawn_inputs = setup_inputs


def setup_inputs(seed=0):
    import zlib

    import numpy as np

    out = dict(_drawn_inputs(seed))
    spreads = {'L0_conv_ln_w': (1.0, 0.6),
     'L0_conv_ln_b': (0.0, 0.8),
     'L0_conv_wg_b': (0.0, 0.8),
     'L0_conv_wrep_b': (0.0, 0.366),
     'L1_conv_gating_bias': (1.0, 0.6),
     'L1_conv_bo': (0.0, 0.376)}
    factors = {'L0_conv_wq': 8.0,
     'L0_conv_wk': 8.0,
     'L0_conv_wv': 8.0,
     'L0_conv_wb': 8.0,
     'L0_conv_wg_w': 8.0,
     'L0_conv_wrep_w': 8.0,
     'L1_conv_Wg': 64.0,
     'L1_conv_nonbatched_bias': 8.0,
     'L1_conv_Wq': 7.773,
     'L1_conv_Wk': 7.727,
     'L1_conv_Wv': 6.232,
     'L1_conv_Wo': 6.239}
    for name, (base, spread) in spreads.items():
        noise = np.random.default_rng([zlib.crc32(name.encode()), seed]).standard_normal(out[name].shape)
        drawn = base * np.exp(spread * noise) if base else spread * noise
        out[name] = jnp.asarray(drawn.astype(out[name].dtype))
    for name, factor in factors.items():
        out[name] = (out[name] * factor).astype(out[name].dtype)
    return out
```

```python
from contextlib import ExitStack

import concourse.bass as bass
from concourse import mybir

ALU = mybir.AluOpType
ACT = mybir.ActivationFunctionType
AX = mybir.AxisListType
F32 = mybir.dt.float32

P = 128
BANK = 512
BIG = 3.0e38
GROUPS = 32
EPS_NORM = 1e-5


def wait(eng, sem, value):
    if isinstance(value, int) and value <= 0:
        return
    eng.wait_ge(sem, value)


def each_row(eng, rows, blk, row):
    n = rows // blk
    row(-1, blk - 1, False, False, True)
    for k in range(blk):
        row(0, k, k > 0, True, True)
    with eng.Fori(1, n - 1) as b:
        for k in range(blk):
            row(b, k, True, True, True)
    for k in range(blk):
        row(n - 1, k, True, True, k < blk - 1)
    row(n, 0, True, False, False)


def two_layers(nc, x, ln_w, ln_b, wq0, wk0, wv0, wg0, wb0, wg0_b, wrep, wrep_b,
               pair_bias1, wq1, wk1, wv1, wg1, wg1_b, wo1, bo1, ident, out):
    C, H, W = x.shape
    JT = W // P
    NH0 = wb0.shape[1]
    D0 = wq0.shape[1] // NH0
    NH1 = pair_bias1.shape[0]
    D1 = wq1.shape[1] // NH1
    D = W
    MT = wq0.shape[1] // P
    GS = W // GROUPS
    COUNT = float(C * H * GS)
    SCALE0 = float(D0) ** -0.5
    SCALE1 = float(D1) ** -0.5
    QR = 4
    CH = QR * W
    NCH = H // QR
    PR = 2
    PW = PR * W
    NP = H // PR
    NR1 = C
    BW = 32

    with ExitStack() as ctx:
        def sb(name, shape, dt=F32):
            return ctx.enter_context(nc.sbuf_tensor(name, shape, dt))

        def sem(name):
            return ctx.enter_context(nc.semaphore(name))

        ps = ctx.enter_context(nc.psum_tensor("ps", [P, 8, BANK], F32))
        psS = [ps[:, b, :].rearrange("p (t k) -> p t k", t=JT) for b in (0, 1)]
        psT = [ps[:, b, :].rearrange("p (t j) -> p t j", t=JT) for b in (2, 3)]
        psJ = [ps[:, b, :].rearrange("p (t j) -> p t j", t=2) for b in (4, 5)]
        psO = [ps[:, b, :] for b in (6, 7)]
        psA = [ps[0:3 * BW, b:b + 2, :] for b in (0, 2)]

        ident_sb = sb("ident_sb", [P, P])
        ones = sb("ones", [P, P])
        wq0_sb, wk0_sb, wv0_sb, wg0_sb = (sb(n, [P, MT * P]) for n in ("wq0_sb", "wk0_sb", "wv0_sb", "wg0_sb"))
        wb0_sb = sb("wb0_sb", [P, BW])
        wrep_sb = sb("wrep_sb", [P, MT, C])
        gb0 = sb("gb0", [P, MT])
        gb1 = sb("gb1", [P, MT])
        rb0 = sb("rb0", [P, 1])
        wq1_sb, wk1_sb, wv1_sb, wg1_sb, wo1_sb = (
            sb(n, [P, MT, D]) for n in ("wq1_sb", "wk1_sb", "wv1_sb", "wg1_sb", "wo1_sb"))
        bo1_sb = sb("bo1_sb", [P, JT, D])
        nbias0 = sb("nbias0", [P, NH0, JT, W])
        nbias1 = sb("nbias1", [P, NH1, JT, W])

        abuf = sb("abuf", [P, 3, 2, CH])
        xa, wa, ba = (abuf[:, a] for a in range(3))
        ya, sq = (sb(n, [P, 2, CH]) for n in ("ya", "sq"))
        prod = sb("prod", [3 * BW, 2, CH])
        sum0 = sb("sum0", [P, 2, CH])
        bias_parts = nc.dram_tensor("bias_parts", [3, NH0, H, W], F32, kind="Internal").ap()

        gsum = sb("gsum", [P, 2, GROUPS])
        gtot = sb("gtot", [P, 2, GROUPS])
        st = sb("st", [P, 8, GROUPS])
        tall = sb("tall", [P, 4])
        mean_r, rstd_r = sb("mean_r", [P, PR, W]), sb("rstd_r", [P, PR, W])
        parts_sb = abuf[:].rearrange("p a n (m t k) -> p a (n m) t k", t=JT, k=W)

        x_in, w_in, b_in, xln, xres, x1 = (
            sb(n, [P, 2, PW]) for n in ("x_in", "w_in", "b_in", "xln", "xres", "x1"))
        sqr = sb("sqr", [P, PW])
        sum1 = sb("sum1", [P, 2, PW])
        q_sb, k_sb, th_sb = (sb(n, [P, 2, MT, W]) for n in ("q_sb", "k_sb", "th_sb"))
        v0_sb = sb("v0_sb", [P, 2, JT, NH0, D0 + 1])
        v1_sb = sb("v1_sb", [P, 2, JT, NH1, D1 + 1])
        p_sb = sb("p_sb", [P, 2, JT, W])
        pT_sb = sb("pT_sb", [P, 2, JT, W])
        nmax = sb("nmax", [P, 2, 2 * NH1])
        rinv = sb("rinv", [P, JT, NH1])
        on_sb = sb("on_sb", [P, JT, MT * P])
        og_sb = sb("og_sb", [P, MT, W])

        r_in, xn, r_b, y_sb = (sb(n, [P, 2, JT, D]) for n in ("r_in", "xn", "r_b", "y_sb"))
        xnT = sb("xnT", [P, MT, W])

        x1_dram = nc.dram_tensor("x1_dram", [C, H, W], F32, kind="Internal").ap()

        sp_seen = sem("sp_seen")
        wb0_in = sem("wb0_in")
        weights_in = sem("weights_in")
        consts_set = sem("consts_set")
        setup_done = sem("setup_done")
        a_loaded = [sem("a_loaded0"), sem("a_loaded1")]
        a_prod, a_sum, a_sq = sem("a_prod"), sem("a_sum"), sem("a_sq")
        a_mm, a_out = sem("a_mm"), sem("a_out")
        a_stored = [sem("a_stored0"), sem("a_stored1")]
        st_step, st_red, st_mm = sem("st_step"), sem("st_red"), sem("st_mm")
        st_var, st_sqrt = sem("st_var"), sem("st_sqrt")
        parts_in, bias_ready = sem("parts_in"), sem("bias_ready")
        stats_ready = [sem("stats_ready0"), sem("stats_ready1")]

        def layer_sems(n):
            names = ("s", "t", "av", "q", "k", "v", "g", "ot", "out", "max", "exp", "qe", "ke", "ve", "ge", "pt",
                     "den", "on", "gate", "fin", "nstep", "ln", "sstep", "res", "xt", "xte", "seen")
            return {k: sem(f"l{n}_{k}") for k in names}

        S0, S1 = layer_sems(0), layer_sems(1)
        c_loaded = [sem("c_loaded0"), sem("c_loaded1")]
        c_stored = [sem("c_stored0"), sem("c_stored1")]
        e_loaded = [sem("e_loaded0"), sem("e_loaded1")]
        e_stored = [sem("e_stored0"), sem("e_stored1")]

        def by_pair(a):
            return a.rearrange("c (p r) j -> p c (r j)", r=PR)

        def by_chunk(a):
            return a.rearrange("c (n r) j -> n c (r j)", r=QR)

        x_c, w_c, b_c = by_chunk(x), by_chunk(ln_w), by_chunk(ln_b)
        x_p, w_p, b_p, x1_p = by_pair(x), by_pair(ln_w), by_pair(ln_b), by_pair(x1_dram)
        parts_c = bias_parts.rearrange("a h (n r) j -> n a h (r j)", r=QR)
        x1_l = x1_dram.rearrange("b (t l) d -> b l t d", t=JT)
        out_l = out.rearrange("b (t l) d -> b l t d", t=JT)

        weight_loads = [
            (ident_sb[:], ident), (wq0_sb[:], wq0), (wk0_sb[:], wk0), (wv0_sb[:], wv0), (wg0_sb[:], wg0),
            (wrep_sb[:], wrep.rearrange("(t p) o -> p t o", p=P)),
            (gb0[:], wg0_b), (gb1[:], wg1_b), (rb0[:], wrep_b),
            (wq1_sb[:], wq1.rearrange("(t p) o -> p t o", p=P)),
            (wk1_sb[:], wk1.rearrange("(t p) o -> p t o", p=P)),
            (wv1_sb[:], wv1.rearrange("(t p) o -> p t o", p=P)),
            (wg1_sb[:], wg1.rearrange("(t p) o -> p t o", p=P)),
            (wo1_sb[:], wo1.rearrange("(t p) o -> p t o", p=P)),
        ]
        weight_loads += [(bo1_sb[:, t, :], bo1.partition_broadcast(P)) for t in range(JT)]
        weight_loads += [(nbias1[:, h], pair_bias1[h].rearrange("(t p) k -> p t k", p=P)) for h in range(NH1)]
        WEIGHTS = 16 * len(weight_loads)
        CONSTS = 5
        SETUP_OPS = 3

        block = ctx.enter_context(nc.Block())

        @block.sync
        def _(sp):
            sp.wait_ge(consts_set, 1)
            sp.dma_start(wb0_sb[:, 0:NH0], wb0).then_inc(wb0_in, 16)

            def load_chunk(n, par):
                wait(sp, a_mm, n - 1)
                sp.sem_inc(sp_seen, 1)
                wait(sp, a_sum, n * 2)
                sp.dma_start(xa[:, par], x_c[n]).then_inc(a_loaded[par], 16)
                sp.dma_start(wa[:, par], w_c[n]).then_inc(a_loaded[par], 16)
                sp.dma_start(ba[:, par], b_c[n]).then_inc(a_loaded[par], 16)

            def store_products(n, par):
                wait(sp, a_out, n + 1)
                for a in range(3):
                    sp.dma_start(parts_c[n, a], prod[a * BW:a * BW + NH0, par]).then_inc(a_stored[par], 16)

            load_chunk(0, 0)
            load_chunk(1, 1)
            for dst, src in weight_loads:
                sp.dma_start(dst, src).then_inc(weights_in, 16)
            with sp.Fori(1, NCH // 2) as i:
                for par in range(2):
                    load_chunk(i * 2 + par, par)
                    store_products(i * 2 + par - 2, par)
            for par in range(2):
                store_products(NCH - 2 + par, par)

            for par in range(2):
                sp.wait_ge(a_stored[par], 48 * (NCH // 2))
            sp.wait_ge(a_sum, NCH * 2 + 2)
            sp.wait_ge(a_mm, NCH)
            for a in range(3):
                for t in range(JT):
                    sp.dma_start(parts_sb[:, a, :, t, :],
                                 bias_parts[a, :, t * P:(t + 1) * P, :].rearrange("h p j -> p h j")
                                 ).then_inc(parts_in, 16)

            def load_pair(p, par):
                wait(sp, S0["res"], p - 1)
                sp.dma_start(x_in[:, par], x_p[p]).then_inc(c_loaded[par], 16)
                sp.dma_start(w_in[:, par], w_p[p]).then_inc(c_loaded[par], 16)
                sp.dma_start(b_in[:, par], b_p[p]).then_inc(c_loaded[par], 16)

            def store_pair(p, par):
                wait(sp, S0["fin"], p * 2 + 2)
                sp.dma_start(x1_p[p], x1[:, par]).then_inc(c_stored[par], 16)

            LAG = 4
            for p in range(LAG):
                load_pair(p, p % 2)
            with sp.Fori(LAG // 2, NP // 2) as i:
                for par in range(2):
                    load_pair(i * 2 + par, par)
                    store_pair(i * 2 + par - LAG, par)
            for p in range(NP - LAG, NP):
                store_pair(p, p % 2)

            for par in range(2):
                sp.wait_ge(c_stored[par], 16 * (NP // 2))

            def load_row(r, par):
                wait(sp, S1["res"], r - 1)
                sp.dma_start(r_in[:, par], x1_l[r]).then_inc(e_loaded[par], 16)

            def store_row(r, par):
                wait(sp, S1["fin"], r + 1)
                sp.dma_start(out_l[r], y_sb[:, par]).then_inc(e_stored[par], 16)

            for r in range(LAG):
                load_row(r, r % 2)
            with sp.Fori(LAG // 2, NR1 // 2) as i:
                for par in range(2):
                    load_row(i * 2 + par, par)
                    store_row(i * 2 + par - LAG, par)
            for r in range(NR1 - LAG, NR1):
                store_row(r, r % 2)
            for par in range(2):
                sp.wait_ge(e_stored[par], 16 * (NR1 // 2))

        @block.gpsimd
        def _(pool):
            nc.gpsimd.memset(wb0_sb[:], 0.0).then_inc(consts_set, 1)
            nc.gpsimd.memset(ones[:], 1.0).then_inc(consts_set, 1)
            nc.gpsimd.memset(v0_sb[:], 2.0).then_inc(consts_set, 1)
            nc.gpsimd.memset(v1_sb[:], 2.0).then_inc(consts_set, 1)
            nc.gpsimd.memset(sum1[:], 0.0).then_inc(consts_set, 1)
            pool.wait_ge(weights_in, WEIGHTS)
            nc.gpsimd.tensor_scalar(nbias1[:], nbias1[:], -1.0, 0.0, ALU.mult, ALU.add).then_inc(setup_done, 1)
            nc.gpsimd.tensor_scalar(gb0[:], gb0[:], 0.5, 0.0, ALU.mult, ALU.add).then_inc(setup_done, 1)
            nc.gpsimd.tensor_scalar(gb1[:], gb1[:], 0.5, 0.0, ALU.mult, ALU.add).then_inc(setup_done, 1)

            mean, rstd = mean_r[:].rearrange("p r j -> p (r j)"), rstd_r[:].rearrange("p r j -> p (r j)")

            def norm_pair(i, par):
                p = i * 2 + par
                pool.wait_ge(c_loaded[par], i * 48 + 48)
                wait(pool, S0["g"], p * 2 - 2)
                nc.gpsimd.tensor_tensor(xln[:, par], x_in[:, par], mean, ALU.subtract).then_inc(S0["nstep"], 1)
                pool.wait_ge(S0["nstep"], p * 3 + 1)
                nc.gpsimd.tensor_tensor(xln[:, par], xln[:, par], rstd, ALU.mult).then_inc(S0["nstep"], 1)
                pool.wait_ge(S0["nstep"], p * 3 + 2)
                nc.gpsimd.tensor_tensor(xln[:, par], xln[:, par], w_in[:, par], ALU.mult).then_inc(S0["nstep"], 1)
                pool.wait_ge(S0["nstep"], p * 3 + 3)
                nc.gpsimd.tensor_tensor(xln[:, par], xln[:, par], b_in[:, par], ALU.add).then_inc(S0["ln"], 1)

            def sum_pair(i, par):
                p = i * 2 + par
                wait(pool, S0["fin"], p * 2 + 2)
                wait(pool, S0["sstep"], p * 3)
                nc.gpsimd.tensor_tensor(sqr[:], x1[:, par], x1[:, par], ALU.mult).then_inc(S0["sstep"], 1)
                nc.gpsimd.tensor_tensor(sum1[:, 0], sum1[:, 0], x1[:, par], ALU.add).then_inc(S0["sstep"], 1)
                pool.wait_ge(S0["sstep"], p * 3 + 1)
                nc.gpsimd.tensor_tensor(sum1[:, 1], sum1[:, 1], sqr[:], ALU.add).then_inc(S0["sstep"], 1)

            def residual_pair(i, par):
                p = i * 2 + par
                wait(pool, S0["fin"], p * 2 - 2)
                pool.sem_inc(S0["seen"], 1)
                nc.gpsimd.tensor_scalar(xres[:, par], x_in[:, par], 1.0, rb0[:, 0:1], ALU.mult, ALU.add
                                        ).then_inc(S0["res"], 1)

            pool.wait_ge(stats_ready[0], 1)
            for par in range(2):
                norm_pair(0, par)
                residual_pair(0, par)
            with pool.Fori(1, NP // 2) as i:
                for par in range(2):
                    norm_pair(i, par)
                    sum_pair(i - 1, par)
                    residual_pair(i, par)
            for par in range(2):
                sum_pair(NP // 2 - 1, par)

            mean1 = mean_r[:, 0:1, :].to_broadcast([P, JT, D])
            rstd1 = rstd_r[:, 0:1, :].to_broadcast([P, JT, D])

            def norm_row(i, par):
                r = i * 2 + par
                pool.wait_ge(e_loaded[par], i * 16 + 16)
                wait(pool, S1["xt"], r - 1)
                nc.gpsimd.tensor_tensor(xn[:, par], r_in[:, par], mean1, ALU.subtract).then_inc(S1["nstep"], 1)
                pool.wait_ge(S1["nstep"], r + 1)
                nc.gpsimd.tensor_tensor(xn[:, par], xn[:, par], rstd1, ALU.mult).then_inc(S1["ln"], 1)

            def residual_row(r, par):
                wait(pool, S1["fin"], r - 1)
                nc.gpsimd.tensor_tensor(r_b[:, par], r_in[:, par], bo1_sb[:], ALU.add).then_inc(S1["res"], 1)

            pool.wait_ge(stats_ready[1], 1)
            norm_row(0, 0)
            norm_row(0, 1)
            residual_row(0, 0)
            with pool.Fori(1, NR1 // 2) as i:
                for par in range(2):
                    norm_row(i, par)
                    residual_row(i * 2 + par - 1, 1 - par)
            residual_row(NR1 - 1, 1)

        @block.tensor
        def _(pe):
            mm = nc.tensor.matmul

            def products(n, i, par):
                wait(pe, a_out, n - 1)
                pe.wait_ge(a_loaded[par], i * 48 + 48)
                pe.wait_ge(a_prod, n + 1)
                for half in range(CH // BANK):
                    cols = slice(half * BANK, (half + 1) * BANK)
                    for a, src in enumerate((ya, wa, ba)):
                        last = mm(psA[par][a * BW:(a + 1) * BW, half, :], wb0_sb[:], src[:, par, cols],
                                  start=True, stop=True)
                last.then_inc(a_mm, 1)

            pe.wait_ge(wb0_in, 16)
            products(0, 0, 0)
            products(1, 0, 1)
            with pe.Fori(1, NCH // 2) as i:
                for par in range(2):
                    products(i * 2 + par, i, par)

            def totals(k):
                pe.wait_ge(st_red, 2 * k + 2)
                mm(ps[:, 4, 0:2 * GROUPS], ones[:], gsum[:].rearrange("p s g -> p (s g)"),
                   start=True, stop=True).then_inc(st_mm, 1)

            pe.wait_ge(consts_set, CONSTS)
            totals(0)
            pe.wait_ge(weights_in, WEIGHTS)
            pe.wait_ge(bias_ready, 1)

            def scores(S, r, h, nh, d, par):
                g = r * nh + h
                if h == 0:
                    pe.wait_ge(S["qe"], r + 1)
                    pe.wait_ge(S["ke"], r + 1)
                wait(pe, S["exp"], g * 2 - 2)
                m, lo = h * d // P, h * d % P
                for t in range(JT):
                    last = mm(psS[h % 2][:, t, :], q_sb[lo:lo + d, par, m, t * P:(t + 1) * P],
                              k_sb[lo:lo + d, par, m, :], start=True, stop=True)
                last.then_inc(S["s"], 1)

            def turn_probs(S, g, h):
                pe.wait_ge(S["exp"], g * 2 + 2)
                wait(pe, S["pt"], g - 1)
                for t in range(JT):
                    for u in range(JT):
                        last = nc.tensor.transpose(psT[h % 2][:, u, t * P:(t + 1) * P],
                                                   p_sb[:, h % 2, t, u * P:(u + 1) * P], ident_sb[:])
                last.then_inc(S["t"], 1)

            def weigh_values(S, r, h, nh, d, v, par):
                g = r * nh + h
                pe.wait_ge(S["pt"], g + 1)
                if h == 0:
                    pe.wait_ge(S["ve"], r + 1)
                    wait(pe, S["on"], r)
                for t in range(JT):
                    for u in range(JT):
                        last = mm(psO[t][:, h * (d + 1):(h + 1) * (d + 1)], pT_sb[:, h % 2, u, t * P:(t + 1) * P],
                                  v[:, par, u, h, :], start=(u == 0), stop=(u == JT - 1))
                last.then_inc(S["av"], 1)

            def turn_outputs(S, r, bank):
                pe.wait_ge(S["on"], r + 1)
                for m in range(MT):
                    for t in range(JT):
                        last = nc.tensor.transpose(psJ[bank][:, m, t * P:(t + 1) * P],
                                                   on_sb[:, t, m * P:(m + 1) * P], ident_sb[:])
                last.then_inc(S["ot"], 1)

            def row0(b, k, prv, cur, nxt):
                r = b * 4 + k
                k1 = (k + 1) % 4
                xr = xln[:, k1 // 2, (k1 % 2) * W:(k1 % 2 + 1) * W]
                for h in range(NH0):
                    if cur:
                        scores(S0, r, h, NH0, D0, k % 2)
                    if nxt and h == 0:
                        if k1 % 2 == 0:
                            pe.wait_ge(S0["ln"], (b + (k == 3)) * 2 + k1 // 2 + 1)
                        wait(pe, S0["ge"], r + 1)
                        for m in range(MT):
                            last = mm(psJ[0][:, m, :], wq0_sb[:, m * P:(m + 1) * P], xr, start=True, stop=True)
                        last.then_inc(S0["q"], 1)
                    if nxt and h == 1:
                        wait(pe, S0["fin"], r - 1)
                        for m in range(MT):
                            last = mm(psJ[1][:, m, :], wk0_sb[:, m * P:(m + 1) * P], xr, start=True, stop=True)
                        last.then_inc(S0["k"], 1)
                    if nxt and h == 2:
                        pe.wait_ge(S0["qe"], r + 2)
                        for t in range(JT):
                            last = mm(psJ[0][:, t, :], xr[:, t * P:(t + 1) * P], wv0_sb[:], start=True, stop=True)
                        last.then_inc(S0["v"], 1)
                    if nxt and h == 3:
                        pe.wait_ge(S0["ve"], r + 2)
                        for m in range(MT):
                            last = mm(psJ[0][:, m, :], wg0_sb[:, m * P:(m + 1) * P], xr, start=True, stop=True)
                        last.then_inc(S0["g"], 1)
                    if (cur and h >= 1) or (prv and h == 0):
                        turn_probs(S0, r * NH0 + h - 1, (h - 1) % 2)
                    if prv and h == 2:
                        if nxt:
                            pe.wait_ge(S0["ke"], r + 2)
                        turn_outputs(S0, r - 1, 1)
                    if cur and h >= 2:
                        weigh_values(S0, r, h - 2, NH0, D0, v0_sb, k % 2)
                    if prv and h < 2:
                        weigh_values(S0, r - 1, NH0 - 2 + h, NH0, D0, v0_sb, (k - 1) % 2)
                    if prv and h == 3:
                        pe.wait_ge(S0["gate"], r)
                        for m in range(MT):
                            last = mm(psJ[1][:, 0, :], wrep_sb[:, m, :], og_sb[:, m, :],
                                      start=(m == 0), stop=(m == MT - 1))
                        last.then_inc(S0["out"], 1)

            each_row(pe, H, 4, row0)

            totals(1)

            def row1(b, k, prv, cur, nxt):
                r = b * 2 + k
                par = (k + 1) % 2
                for h in range(NH1):
                    if cur:
                        scores(S1, r, h, NH1, D1, k % 2)
                    if nxt and h == 0:
                        pe.wait_ge(S1["ln"], r + 2)
                        wait(pe, S1["fin"], r - 1)
                        for m in range(MT):
                            for t in range(JT):
                                last = nc.tensor.transpose(psJ[0][:, m, t * P:(t + 1) * P],
                                                           xn[:, par, t, m * P:(m + 1) * P], ident_sb[:])
                        last.then_inc(S1["xt"], 1)
                    if nxt and h == 1:
                        pe.wait_ge(S1["xte"], r + 2)
                        wait(pe, S1["ge"], r + 1)
                        for m in range(MT):
                            for c in range(MT):
                                last = mm(psJ[1][:, m, :], wq1_sb[:, c, m * P:(m + 1) * P], xnT[:, c, :],
                                          start=(c == 0), stop=(c == MT - 1))
                        last.then_inc(S1["q"], 1)
                    if nxt and h == 2:
                        for m in range(MT):
                            for c in range(MT):
                                last = mm(psJ[0][:, m, :], wk1_sb[:, c, m * P:(m + 1) * P], xnT[:, c, :],
                                          start=(c == 0), stop=(c == MT - 1))
                        last.then_inc(S1["k"], 1)
                    if nxt and h == 3:
                        pe.wait_ge(S1["qe"], r + 2)
                        for t in range(JT):
                            for c in range(MT):
                                last = mm(psJ[1][:, t, :], xnT[:, c, t * P:(t + 1) * P], wv1_sb[:, c, :],
                                          start=(c == 0), stop=(c == MT - 1))
                        last.then_inc(S1["v"], 1)
                    if nxt and h == 4:
                        pe.wait_ge(S1["ve"], r + 2)
                        for m in range(MT):
                            for c in range(MT):
                                last = mm(psJ[1][:, m, :], wg1_sb[:, c, m * P:(m + 1) * P], xnT[:, c, :],
                                          start=(c == 0), stop=(c == MT - 1))
                        last.then_inc(S1["g"], 1)
                    if (cur and h >= 1) or (prv and h == 0):
                        turn_probs(S1, r * NH1 + h - 1, (h - 1) % 2)
                    if prv and h == 3:
                        if nxt:
                            pe.wait_ge(S1["ke"], r + 2)
                        turn_outputs(S1, r - 1, 0)
                    if cur and h >= 2:
                        weigh_values(S1, r, h - 2, NH1, D1, v1_sb, k % 2)
                    if prv and h < 2:
                        weigh_values(S1, r - 1, NH1 - 2 + h, NH1, D1, v1_sb, (k - 1) % 2)
                    if prv and h == 5:
                        pe.wait_ge(S1["gate"], r)
                        for t in range(JT):
                            for m in range(MT):
                                last = mm(psJ[0][:, t, :], og_sb[:, m, t * P:(t + 1) * P], wo1_sb[:, m, :],
                                          start=(m == 0), stop=(m == MT - 1))
                        last.then_inc(S1["out"], 1)

            pe.wait_ge(stats_ready[1], 1)
            each_row(pe, NR1, 2, row1)

        @block.scalar
        def _(act):
            def chunk(n, i, par):
                act.wait_ge(a_loaded[par], i * 48 + 48)
                wait(act, a_sum, n * 2)
                nc.scalar.activation(sq[:, par], xa[:, par], ACT.Square).then_inc(a_sq, 1)
                act.wait_ge(a_mm, n + 1)
                wait(act, a_stored[par], i * 48)
                nc.scalar.activation(prod[:, par].rearrange("p (h n) -> p h n", n=BANK), psA[par],
                                     ACT.Copy).then_inc(a_out, 1)

            chunk(0, 0, 0)
            chunk(1, 0, 1)
            with act.Fori(1, NCH // 2) as i:
                for par in range(2):
                    chunk(i * 2 + par, i, par)

            def sqrt_of(col, n, count):
                act.wait_ge(st_var, count)
                nc.scalar.activation(st[:, col, 0:n], st[:, col - 1, 0:n], ACT.Sqrt).then_inc(st_sqrt, 1)

            sqrt_of(1, GROUPS, 1)
            sqrt_of(5, 1, 2)
            act.wait_ge(setup_done, SETUP_OPS)

            def exponentials(S, r, h, nh, par):
                act.wait_ge(S["max"], r * nh + h + 1)
                for t in range(JT):
                    nc.scalar.activation(p_sb[:, h % 2, t, :], psS[h % 2][:, t, :], ACT.Exp,
                                         bias=nmax[:, par, 2 * h + t:2 * h + t + 1], scale=-1.0
                                         ).then_inc(S["exp"], 1)

            def copy_turned(S, g, h):
                act.wait_ge(S["t"], g + 1)
                nc.scalar.activation(pT_sb[:, h % 2], psT[h % 2], ACT.Copy).then_inc(S["pt"], 1)

            def gates(S, r, bank, par, half_bias):
                act.wait_ge(S["g"], r + 1)
                wait(act, S["gate"], r - 1)
                for m in range(MT):
                    last = nc.scalar.activation(th_sb[:, par, m, :], psJ[bank][:, m, :], ACT.Tanh,
                                                bias=half_bias[:, m:m + 1], scale=0.5)
                last.then_inc(S["ge"], 1)

            def row0(b, k, prv, cur, nxt):
                r = b * 4 + k
                par = (k + 1) % 2
                for h in range(NH0):
                    if cur:
                        exponentials(S0, r, h, NH0, k % 2)
                    if nxt and h == 0:
                        act.wait_ge(S0["q"], r + 2)
                        nc.scalar.activation(q_sb[:, par], psJ[0], ACT.Copy, scale=-SCALE0).then_inc(S0["qe"], 1)
                    if nxt and h == 1:
                        act.wait_ge(S0["k"], r + 2)
                        nc.scalar.activation(k_sb[:, par], psJ[1], ACT.Copy).then_inc(S0["ke"], 1)
                    if nxt and h == 3:
                        gates(S0, r + 1, 0, par, gb0)
                    if (cur and h >= 1) or (prv and h == 0):
                        copy_turned(S0, r * NH0 + h - 1, (h - 1) % 2)

            each_row(act, H, 4, row0)

            sqrt_of(1, GROUPS, 3)

            def row1(b, k, prv, cur, nxt):
                r = b * 2 + k
                par = (k + 1) % 2
                for h in range(NH1):
                    if cur:
                        exponentials(S1, r, h, NH1, k % 2)
                    if nxt and h == 1:
                        act.wait_ge(S1["q"], r + 2)
                        nc.scalar.activation(q_sb[:, par], psJ[1], ACT.Copy, scale=-SCALE1).then_inc(S1["qe"], 1)
                    if nxt and h == 2:
                        act.wait_ge(S1["k"], r + 2)
                        nc.scalar.activation(k_sb[:, par], psJ[0], ACT.Copy).then_inc(S1["ke"], 1)
                    if nxt and h == 4:
                        gates(S1, r + 1, 1, par, gb1)
                    if (cur and h >= 1) or (prv and h == 0):
                        copy_turned(S1, r * NH1 + h - 1, (h - 1) % 2)

            each_row(act, NR1, 2, row1)

        @block.vector
        def _(dve):
            nc.vector.memset(sum0[:], 0.0).then_inc(a_sum, 2)

            def chunk(n, i, par):
                dve.wait_ge(a_loaded[par], i * 48 + 48)
                wait(dve, a_mm, n - 1)
                nc.vector.tensor_tensor(ya[:, par], xa[:, par], wa[:, par], ALU.mult).then_inc(a_prod, 1)
                dve.wait_ge(a_sum, n * 2 + 2)
                nc.vector.tensor_tensor(sum0[:, 0], sum0[:, 0], xa[:, par], ALU.add).then_inc(a_sum, 1)
                dve.wait_ge(a_sq, n + 1)
                nc.vector.tensor_tensor(sum0[:, 1], sum0[:, 1], sq[:, par], ALU.add).then_inc(a_sum, 1)

            chunk(0, 0, 0)
            chunk(1, 0, 1)
            with dve.Fori(1, NCH // 2) as i:
                for par in range(2):
                    chunk(i * 2 + par, i, par)

            done = [0]

            def then(instruction):
                done[0] += 1
                instruction.then_inc(st_step, 1)
                dve.wait_ge(st_step, done[0])

            v = nc.vector
            mean, ex2, var = st[:, 6, :], st[:, 7, :], st[:, 0, :]

            def inverse_root(col, n, to):
                a, root, t = st[:, col, 0:n], st[:, col + 1, 0:n], st[:, col + 2, 0:n]
                then(v.reciprocal(to, root))
                then(v.tensor_tensor(t, to, to, ALU.mult))
                then(v.tensor_tensor(t, t, a, ALU.mult))
                then(v.tensor_scalar(t, t, -0.5, 1.5, ALU.mult, ALU.add))
                then(v.tensor_tensor(to, to, t, ALU.mult))

            def group_stats(sums, rows, k):
                for s in range(2):
                    v.tensor_reduce(gsum[:, s, :], sums[:, s, :].rearrange("p (r g e) -> p g r e", r=rows, e=GS),
                                    AX.XY, ALU.add).then_inc(st_red, 1)
                dve.wait_ge(st_mm, k + 1)
                then(v.tensor_scalar(st[:, 6:8, :], ps[:, 4, 0:2 * GROUPS].rearrange("p (s g) -> p s g", s=2),
                                     1.0 / COUNT, None, ALU.mult))
                then(v.tensor_tensor(st[:, 3, :], mean, mean, ALU.mult))
                then(v.tensor_tensor(st[:, 3, :], ex2, st[:, 3, :], ALU.subtract))
                then(v.tensor_scalar(st[:, 3, :], st[:, 3, :], 0.0, None, ALU.max))

            dve.wait_ge(a_sum, NCH * 2 + 2)
            group_stats(sum0, QR, 0)
            v.tensor_scalar(var, st[:, 3, :], EPS_NORM, None, ALU.add).then_inc(st_var, 1)
            dve.wait_ge(st_var, 1)
            dve.wait_ge(st_sqrt, 1)
            gr = gtot[:, 0, :]
            inverse_root(0, GROUPS, gr)
            then(v.tensor_tensor(st[:, 2, :], gr, gr, ALU.mult))
            then(v.tensor_tensor(st[:, 2, :], st[:, 2, :], st[:, 3, :], ALU.mult))
            then(v.tensor_reduce(tall[:, 0:1], st[:, 2, :], AX.X, ALU.add))
            v.tensor_scalar(st[:, 4, 0:1], tall[:, 0:1], 1.0 / GROUPS, EPS_NORM, ALU.mult, ALU.add
                            ).then_inc(st_var, 1)
            dve.wait_ge(st_var, 2)
            dve.wait_ge(st_sqrt, 2)
            inverse_root_1 = tall[:, 1:2]
            then(v.reciprocal(inverse_root_1, st[:, 5, 0:1]))
            then(v.tensor_tensor(tall[:, 2:3], inverse_root_1, inverse_root_1, ALU.mult))
            then(v.tensor_tensor(tall[:, 2:3], tall[:, 2:3], st[:, 4, 0:1], ALU.mult))
            then(v.tensor_scalar(tall[:, 2:3], tall[:, 2:3], -0.5, 1.5, ALU.mult, ALU.add))
            then(v.tensor_tensor(inverse_root_1, inverse_root_1, tall[:, 2:3], ALU.mult))
            then(v.tensor_scalar(gr, gr, inverse_root_1, None, ALU.mult))

            def spread(r):
                for dst, src in ((mean_r, mean), (rstd_r, gr)):
                    then(v.tensor_copy(dst[:, r, :].rearrange("p (g e) -> p g e", e=GS),
                                       src.unsqueeze(2).to_broadcast([P, GROUPS, GS])))

            for r in range(PR):
                spread(r)
            dve.wait_ge(parts_in, 16 * 3 * JT)
            parts = [parts_sb[:, a].rearrange("p h t k -> p (h t) k") for a in range(3)]
            wide = [P, NH0 * JT, W]
            then(v.tensor_tensor(parts[1], parts[1], mean_r[:, 0:1, :].to_broadcast(wide), ALU.mult))
            then(v.tensor_tensor(parts[0], parts[0], parts[1], ALU.subtract))
            then(v.tensor_tensor(parts[0], parts[0], rstd_r[:, 0:1, :].to_broadcast(wide), ALU.mult))
            flat = [parts_sb[:, a].rearrange("p h t k -> p (h t k)") for a in (0, 2)]
            v.scalar_tensor_tensor(out=nbias0[:].rearrange("p h t k -> p (h t k)"), in0=flat[0], scalar=-1.0,
                                   in1=flat[1], op0=ALU.mult, op1=ALU.subtract).then_inc(bias_ready, 1)
            dve.wait_ge(bias_ready, 1)
            v.tensor_copy(tall[:, 3:4], tall[:, 1:2]).then_inc(stats_ready[0], 1)
            dve.wait_ge(setup_done, SETUP_OPS)
            dve.wait_ge(consts_set, CONSTS)

            def bias_and_max(S, r, h, nh, par, nbias):
                dve.wait_ge(S["s"], r * nh + h + 1)
                dve.sem_inc(S["seen"], 1)
                for t in range(JT):
                    last = v.tensor_tensor_reduce(psS[h % 2][:, t, :], psS[h % 2][:, t, :], nbias[:, h, t, :], 1.0, BIG,
                                           ALU.add, ALU.min, nmax[:, par, 2 * h + t:2 * h + t + 1])
                last.then_inc(S["max"], 1)

            def divide(S, r, nh, d):
                dve.wait_ge(S["av"], (r + 1) * nh)
                o = [psO[t][:, 0:nh * (d + 1)].rearrange("p (h e) -> p h e", e=d + 1) for t in range(JT)]
                for t in range(JT):
                    v.reciprocal(rinv[:, t, 0:nh], o[t][:, :, d]).then_inc(S["den"], 1)
                for t in range(JT):
                    dve.wait_ge(S["den"], r * 2 + 2)
                    last = v.tensor_tensor(on_sb[:, t, :].rearrange("p (h e) -> p h e", e=d), o[t][:, :, 0:d],
                                           rinv[:, t, 0:nh].unsqueeze(2).to_broadcast([P, nh, d]), ALU.mult)
                last.then_inc(S["on"], 1)

            def apply_gates(S, r, bank, par):
                dve.wait_ge(S["ot"], r + 1)
                dve.wait_ge(S["ge"], r + 1)
                v.scalar_tensor_tensor(out=og_sb[:].rearrange("p m j -> p (m j)"),
                                       in0=th_sb[:, par].rearrange("p m j -> p (m j)"), scalar=1.0,
                                       in1=psJ[bank].rearrange("p m j -> p (m j)"),
                                       op0=ALU.add, op1=ALU.mult).then_inc(S["gate"], 1)

            def copy_values(S, r, bank, par, v_sb, d):
                dve.wait_ge(S["v"], r + 1)
                v.tensor_copy(v_sb[:, par, :, :, 0:d], psJ[bank].rearrange("p t (h e) -> p t h e", e=d)
                              ).then_inc(S["ve"], 1)

            def row0(b, k, prv, cur, nxt):
                r = b * 4 + k
                for h in range(NH0):
                    if prv and h == 2:
                        divide(S0, r - 1, NH0, D0)
                    if prv and h == 3:
                        apply_gates(S0, r - 1, 1, (k - 1) % 2)
                    if cur:
                        bias_and_max(S0, r, h, NH0, k % 2, nbias0)
                    if nxt and h == 2:
                        copy_values(S0, r + 1, 0, (k + 1) % 2, v0_sb, D0)
                    if prv and h == 3:
                        kp = (k - 1) % 4
                        pair, half = kp // 2, kp % 2
                        dve.wait_ge(S0["out"], r)
                        if half == 0:
                            i = b - (k == 0)
                            dve.wait_ge(S0["res"], i * 2 + pair + 1)
                            wait(dve, S0["sstep"], (i * 2 + pair - 1) * 3)
                            wait(dve, c_stored[pair], i * 16)
                        v.tensor_tensor(x1[:, pair, half * W:(half + 1) * W], psJ[1][:, 0, :],
                                        xres[:, pair, half * W:(half + 1) * W], ALU.add).then_inc(S0["fin"], 1)

            each_row(dve, H, 4, row0)

            dve.wait_ge(S0["sstep"], NP * 3)
            group_stats(sum1, PR, 1)
            v.tensor_scalar(var, st[:, 3, :], EPS_NORM, None, ALU.add).then_inc(st_var, 1)
            dve.wait_ge(st_var, 3)
            dve.wait_ge(st_sqrt, 3)
            inverse_root(0, GROUPS, gr)
            spread(0)
            v.tensor_copy(tall[:, 3:4], gr[:, 0:1]).then_inc(stats_ready[1], 1)

            def row1(b, k, prv, cur, nxt):
                r = b * 2 + k
                for h in range(NH1):
                    if prv and h == 2:
                        divide(S1, r - 1, NH1, D1)
                    if prv and h == 4:
                        apply_gates(S1, r - 1, 0, (k - 1) % 2)
                    if cur:
                        bias_and_max(S1, r, h, NH1, k % 2, nbias1)
                    if nxt and h == 0:
                        dve.wait_ge(S1["xt"], r + 2)
                        v.tensor_copy(xnT[:], psJ[0]).then_inc(S1["xte"], 1)
                    if nxt and h == 3:
                        copy_values(S1, r + 1, 1, (k + 1) % 2, v1_sb, D1)
                    if prv and h == 5:
                        par = (k - 1) % 2
                        dve.wait_ge(S1["out"], r)
                        dve.wait_ge(S1["res"], r)
                        wait(dve, e_stored[par], (b - (k == 0)) * 16)
                        v.tensor_tensor(y_sb[:, par], psJ[0], r_b[:, par], ALU.add).then_inc(S1["fin"], 1)

            each_row(dve, NR1, 2, row1)


def kernel(**inputs):
    import numpy as _np
    import concourse.bacc as _bacc
    from concourse import mybir as _mybir
    from concourse.bass_utils import run_bass_kernel_spmd as _run

    def a(name):
        return _np.asarray(inputs[name])

    C, H, W = a("x").shape[1:]
    nh0 = a("L0_conv_wb").shape[0]
    hc0 = a("L0_conv_wq").shape[0]
    given = {
        "x": a("x")[0], "ln_w": a("L0_conv_ln_w"), "ln_b": a("L0_conv_ln_b"),
        "wq0": a("L0_conv_wq").T, "wk0": a("L0_conv_wk").T, "wv0": a("L0_conv_wv").T, "wg0": a("L0_conv_wg_w").T,
        "wb0": a("L0_conv_wb").T, "wg0_b": a("L0_conv_wg_b").reshape(-1, 128).T,
        "wrep": a("L0_conv_wrep_w").reshape(C, hc0 // nh0, nh0).transpose(2, 1, 0).reshape(hc0, C),
        "wrep_b": a("L0_conv_wrep_b").reshape(C, 1),
        "pair_bias1": a("L1_conv_nonbatched_bias")[0],
        "wq1": a("L1_conv_Wq").T, "wk1": a("L1_conv_Wk").T, "wv1": a("L1_conv_Wv").T, "wg1": a("L1_conv_Wg").T,
        "wg1_b": a("L1_conv_gating_bias").reshape(-1, 128).T,
        "wo1": a("L1_conv_Wo").T, "bo1": a("L1_conv_bo"),
        "ident": _np.eye(128, dtype=_np.float32),
    }
    nc = _bacc.Bacc("TRN2", target_bir_lowering=False, num_devices=1)
    arrays, args = {}, []
    for name, array in given.items():
        array = _np.ascontiguousarray(array)
        arrays[f"in_{name}_dram"] = array
        args.append(nc.dram_tensor(f"in_{name}_dram", array.shape, _mybir.dt.from_np(array.dtype),
                                   kind="ExternalInput").ap())
    args.append(nc.dram_tensor("out_0_dram", (C, H, W), _mybir.dt.float32, kind="ExternalOutput").ap())
    two_layers(nc, *args)
    r = _run(nc, [arrays], core_ids=[0])
    return r.results[0]["out_0_dram"].reshape(1, C, H, W)
```

```python
from contextlib import ExitStack

import concourse.bass as bass
from concourse import mybir

ALU = mybir.AluOpType
ACT = mybir.ActivationFunctionType
AX = mybir.AxisListType
F32 = mybir.dt.float32
F16 = mybir.dt.float16

P = 128
BANK = 512
BIG = 3.0e38
GROUPS = 32
EPS_NORM = 1e-5


def wait(eng, sem, value):
    if isinstance(value, int) and value <= 0:
        return
    eng.wait_ge(sem, value)


def each_row(eng, rows, blk, row):
    n = rows // blk
    row(-1, blk - 1, False, False, True)
    for k in range(blk):
        row(0, k, k > 0, True, True)
    with eng.Fori(1, n - 1) as b:
        for k in range(blk):
            row(b, k, True, True, True)
    for k in range(blk):
        row(n - 1, k, True, True, k < blk - 1)
    row(n, 0, True, False, False)


def two_layers(nc, x, ln_w, ln_b, wq0, wk0, wv0, wg0, wb0, wg0_b, wrep, wrep_b,
               pair_bias1, wq1, wk1, wv1, wg1, wg1_b, wo1, bo1, ident, out):
    C, H, W = x.shape
    JT = W // P
    NH0 = wb0.shape[1]
    D0 = wq0.shape[1] // NH0
    NH1 = pair_bias1.shape[0]
    D1 = wq1.shape[1] // NH1
    D = W
    MT = wq0.shape[1] // P
    GS = W // GROUPS
    COUNT = float(C * H * GS)
    SCALE0 = float(D0) ** -0.5
    SCALE1 = float(D1) ** -0.5
    QR = 4
    CH = QR * W
    NCH = H // QR
    PR = 2
    PW = PR * W
    NP = H // PR
    NR1 = C
    BW = 32

    with ExitStack() as ctx:
        def sb(name, shape, dt=F32):
            return ctx.enter_context(nc.sbuf_tensor(name, shape, dt))

        def sem(name):
            return ctx.enter_context(nc.semaphore(name))

        ps = ctx.enter_context(nc.psum_tensor("ps", [P, 8, BANK], F32))
        psS = [ps[:, b, :].rearrange("p (t k) -> p t k", t=JT) for b in (0, 1)]
        psT = [ps[:, b, :].rearrange("p (t j) -> p t j", t=JT) for b in (2, 3)]
        psJ = [ps[:, b, :].rearrange("p (t j) -> p t j", t=2) for b in (4, 5, 6)]
        psO = ps[:, 7, :].rearrange("p (m j) -> p m j", m=2)
        psA = [ps[0:3 * BW, b:b + 2, :] for b in (0, 2)]

        ident_sb = sb("ident_sb", [P, P])
        ones = sb("ones", [P, P])
        wq0_sb, wk0_sb, wv0_sb, wg0_sb = (sb(n, [P, MT * P]) for n in ("wq0_sb", "wk0_sb", "wv0_sb", "wg0_sb"))
        wb0_sb = sb("wb0_sb", [P, BW])
        wrep_sb = sb("wrep_sb", [P, MT, C])
        gb0 = sb("gb0", [P, MT])
        gb1 = sb("gb1", [P, MT])
        rb0 = sb("rb0", [P, 1])
        wq1_sb, wk1_sb, wv1_sb, wg1_sb, wo1_sb = (
            sb(n, [P, MT, D]) for n in ("wq1_sb", "wk1_sb", "wv1_sb", "wg1_sb", "wo1_sb"))
        split0 = {n: sb(f"{n}0_parts", [P, 2, MT * P], F16) for n in "qkvg"}
        split1 = {n: sb(f"{n}1_parts", [P, 2, MT, D], F16) for n in "qkvg"}
        bo1_sb = sb("bo1_sb", [P, JT, D])
        nbias0 = sb("nbias0", [P, NH0, JT, W])
        nbias1 = sb("nbias1", [P, NH1, JT, W])

        abuf = sb("abuf", [P, 3, 2, CH])
        xa, wa, ba = (abuf[:, a] for a in range(3))
        ya, sq = (sb(n, [P, 2, CH]) for n in ("ya", "sq"))
        prod = sb("prod", [3 * BW, 2, CH])
        sum0 = sb("sum0", [P, 2, CH])
        bias_parts = nc.dram_tensor("bias_parts", [3, NH0, H, W], F32, kind="Internal").ap()

        gsum = sb("gsum", [P, 2, GROUPS])
        gtot = sb("gtot", [P, 2, GROUPS])
        st = sb("st", [P, 8, GROUPS])
        tall = sb("tall", [P, 4])
        mean_r, rstd_r = sb("mean_r", [P, PR, W]), sb("rstd_r", [P, PR, W])
        parts_sb = abuf[:].rearrange("p a n (m t k) -> p a (n m) t k", t=JT, k=W)

        x_in, w_in, b_in, xln, xres, x1 = (
            sb(n, [P, 2, PW]) for n in ("x_in", "w_in", "b_in", "xln", "xres", "x1"))
        sqr = sb("sqr", [P, PW])
        sum1 = sb("sum1", [P, 2, PW])
        xparts = sb("xparts", [P, 2, 2, PW], F16)
        q_sb, k_sb = (sb(n, [P, 2, 2, MT, W], F16) for n in ("q_sb", "k_sb"))
        th_sb = sb("th_sb", [P, 2, MT, W])
        v_sb = sb("v_sb", [P, 2, JT, MT * P])
        p_sb = sb("p_sb", [P, 2, JT, W])
        pT_sb = sb("pT_sb", [P, NH1, JT, W])
        nmax = sb("nmax", [P, 2, 2 * NH1])
        rsum = sb("rsum", [P, 2, 2 * NH1])
        rinv = sb("rinv", [P, 2 * NH1])
        rwide = sb("rwide", [P, JT, MT * P])
        gr_sb = sb("gr_sb", [P, MT, W])
        og_sb = sb("og_sb", [P, MT, W])

        r_in, xn, r_b, y_sb = (buf[:, n].rearrange("p (b t d) -> p b t d", b=2, t=JT)
                               for buf in (ya, sq) for n in range(2))
        xnT = sb("xnT", [P, 2, MT, W], F16)

        x1_dram = nc.dram_tensor("x1_dram", [C, H, W], F32, kind="Internal").ap()

        sp_seen = sem("sp_seen")
        wb0_in = sem("wb0_in")
        weights_in = sem("weights_in")
        consts_set = sem("consts_set")
        setup_done = sem("setup_done")
        split_step = sem("split_step")
        a_loaded = [sem("a_loaded0"), sem("a_loaded1")]
        a_prod, a_sum, a_sq = sem("a_prod"), sem("a_sum"), sem("a_sq")
        a_mm, a_out = sem("a_mm"), sem("a_out")
        a_stored = [sem("a_stored0"), sem("a_stored1")]
        st_step, st_red, st_mm = sem("st_step"), sem("st_red"), sem("st_mm")
        st_var, st_sqrt = sem("st_var"), sem("st_sqrt")
        parts_in, bias_ready = sem("parts_in"), sem("bias_ready")
        stats_ready = [sem("stats_ready0"), sem("stats_ready1")]

        def layer_sems(n):
            names = ("s", "t", "av", "q", "k", "v", "g", "r", "out", "max", "exp", "qh", "qe", "kh", "ke", "ve", "ge",
                     "pt", "den", "wide", "gr", "gate", "fin", "xh", "nstep", "ln", "sstep", "res", "xt", "xte", "seen")
            return {k: sem(f"l{n}_{k}") for k in names}

        S0, S1 = layer_sems(0), layer_sems(1)
        c_loaded = [sem("c_loaded0"), sem("c_loaded1")]
        c_stored = [sem("c_stored0"), sem("c_stored1")]
        e_loaded = [sem("e_loaded0"), sem("e_loaded1")]
        e_stored = [sem("e_stored0"), sem("e_stored1")]

        def by_pair(a):
            return a.rearrange("c (p r) j -> p c (r j)", r=PR)

        def by_chunk(a):
            return a.rearrange("c (n r) j -> n c (r j)", r=QR)

        x_c, w_c, b_c = by_chunk(x), by_chunk(ln_w), by_chunk(ln_b)
        x_p, w_p, b_p, x1_p = by_pair(x), by_pair(ln_w), by_pair(ln_b), by_pair(x1_dram)
        parts_c = bias_parts.rearrange("a h (n r) j -> n a h (r j)", r=QR)
        x1_l = x1_dram.rearrange("b (t l) d -> b l t d", t=JT)
        out_l = out.rearrange("b (t l) d -> b l t d", t=JT)

        weight_loads = [
            (ident_sb[:], ident), (wq0_sb[:], wq0), (wk0_sb[:], wk0), (wv0_sb[:], wv0), (wg0_sb[:], wg0),
            (wrep_sb[:], wrep.rearrange("(t p) o -> p t o", p=P)),
            (gb0[:], wg0_b), (gb1[:], wg1_b), (rb0[:], wrep_b),
            (wq1_sb[:], wq1.rearrange("(t p) o -> p t o", p=P)),
            (wk1_sb[:], wk1.rearrange("(t p) o -> p t o", p=P)),
            (wv1_sb[:], wv1.rearrange("(t p) o -> p t o", p=P)),
            (wg1_sb[:], wg1.rearrange("(t p) o -> p t o", p=P)),
            (wo1_sb[:], wo1.rearrange("(t p) o -> p t o", p=P)),
        ]
        weight_loads += [(bo1_sb[:, t, :], bo1.partition_broadcast(P)) for t in range(JT)]
        weight_loads += [(nbias1[:, h], pair_bias1[h].rearrange("(t p) k -> p t k", p=P)) for h in range(NH1)]
        WEIGHTS = 16 * len(weight_loads)
        CONSTS = 3
        SETUP_OPS = 4

        block = ctx.enter_context(nc.Block())

        @block.sync
        def _(sp):
            sp.wait_ge(consts_set, 1)
            sp.dma_start(wb0_sb[:, 0:NH0], wb0).then_inc(wb0_in, 16)

            def load_chunk(n, par):
                wait(sp, a_mm, n - 1)
                sp.sem_inc(sp_seen, 1)
                wait(sp, a_sum, n * 2)
                sp.dma_start(xa[:, par], x_c[n]).then_inc(a_loaded[par], 16)
                sp.dma_start(wa[:, par], w_c[n]).then_inc(a_loaded[par], 16)
                sp.dma_start(ba[:, par], b_c[n]).then_inc(a_loaded[par], 16)

            def store_products(n, par):
                wait(sp, a_out, n + 1)
                for a in range(3):
                    sp.dma_start(parts_c[n, a], prod[a * BW:a * BW + NH0, par]).then_inc(a_stored[par], 16)

            load_chunk(0, 0)
            load_chunk(1, 1)
            for dst, src in weight_loads:
                sp.dma_start(dst, src).then_inc(weights_in, 16)
            with sp.Fori(1, NCH // 2) as i:
                for par in range(2):
                    load_chunk(i * 2 + par, par)
                    store_products(i * 2 + par - 2, par)
            for par in range(2):
                store_products(NCH - 2 + par, par)

            for par in range(2):
                sp.wait_ge(a_stored[par], 48 * (NCH // 2))
            sp.wait_ge(a_sum, NCH * 2 + 2)
            sp.wait_ge(a_mm, NCH)
            for a in range(3):
                for t in range(JT):
                    sp.dma_start(parts_sb[:, a, :, t, :],
                                 bias_parts[a, :, t * P:(t + 1) * P, :].rearrange("h p j -> p h j")
                                 ).then_inc(parts_in, 16)

            def load_pair(p, par):
                wait(sp, S0["res"], p - 1)
                sp.dma_start(x_in[:, par], x_p[p]).then_inc(c_loaded[par], 16)
                sp.dma_start(w_in[:, par], w_p[p]).then_inc(c_loaded[par], 16)
                sp.dma_start(b_in[:, par], b_p[p]).then_inc(c_loaded[par], 16)

            def store_pair(p, par):
                wait(sp, S0["fin"], p * 2 + 2)
                sp.dma_start(x1_p[p], x1[:, par]).then_inc(c_stored[par], 16)

            LAG = 4
            for p in range(LAG):
                load_pair(p, p % 2)
            with sp.Fori(LAG // 2, NP // 2) as i:
                for par in range(2):
                    load_pair(i * 2 + par, par)
                    store_pair(i * 2 + par - LAG, par)
            for p in range(NP - LAG, NP):
                store_pair(p, p % 2)

            for par in range(2):
                sp.wait_ge(c_stored[par], 16 * (NP // 2))

            def load_row(r, par):
                wait(sp, S1["res"], r - 1)
                sp.dma_start(r_in[:, par], x1_l[r]).then_inc(e_loaded[par], 16)

            def store_row(r, par):
                wait(sp, S1["fin"], r + 1)
                sp.dma_start(out_l[r], y_sb[:, par]).then_inc(e_stored[par], 16)

            for r in range(LAG):
                load_row(r, r % 2)
            with sp.Fori(LAG // 2, NR1 // 2) as i:
                for par in range(2):
                    load_row(i * 2 + par, par)
                    store_row(i * 2 + par - LAG, par)
            for r in range(NR1 - LAG, NR1):
                store_row(r, r % 2)
            for par in range(2):
                sp.wait_ge(e_stored[par], 16 * (NR1 // 2))

        @block.gpsimd
        def _(pool):
            nc.gpsimd.memset(wb0_sb[:], 0.0).then_inc(consts_set, 1)
            nc.gpsimd.memset(ones[:], 1.0).then_inc(consts_set, 1)
            nc.gpsimd.memset(sum1[:], 0.0).then_inc(consts_set, 1)
            pool.wait_ge(weights_in, WEIGHTS)
            nc.gpsimd.tensor_scalar(nbias1[:], nbias1[:], -1.0, 0.0, ALU.mult, ALU.add).then_inc(setup_done, 1)
            nc.gpsimd.tensor_scalar(gb0[:], gb0[:], 0.5, 0.0, ALU.mult, ALU.add).then_inc(setup_done, 1)
            nc.gpsimd.tensor_scalar(gb1[:], gb1[:], 0.5, 0.0, ALU.mult, ALU.add).then_inc(setup_done, 1)
            nc.gpsimd.tensor_scalar(wv0_sb[:], wv0_sb[:], 0.5, 0.0, ALU.mult, ALU.add).then_inc(split_step, 1)
            nc.gpsimd.tensor_scalar(wv1_sb[:], wv1_sb[:], 0.5, 0.0, ALU.mult, ALU.add).then_inc(split_step, 1)
            pool.wait_ge(split_step, 2)
            whole = [(wq0_sb, split0["q"]), (wk0_sb, split0["k"]), (wv0_sb, split0["v"]), (wg0_sb, split0["g"]),
                     (wq1_sb, split1["q"]), (wk1_sb, split1["k"]), (wv1_sb, split1["v"]), (wg1_sb, split1["g"])]
            for w, parts in whole:
                nc.gpsimd.tensor_scalar(parts[:, 0], w[:], 1.0, 0.0, ALU.mult, ALU.add).then_inc(split_step, 1)
            pool.wait_ge(split_step, 2 + len(whole))
            for w, parts in whole:
                last = nc.gpsimd.tensor_tensor(parts[:, 1], w[:], parts[:, 0], ALU.subtract)
            last.then_inc(setup_done, 1)

            mean, rstd = mean_r[:].rearrange("p r j -> p (r j)"), rstd_r[:].rearrange("p r j -> p (r j)")

            def norm_pair(i, par):
                p = i * 2 + par
                pool.wait_ge(c_loaded[par], i * 48 + 48)
                wait(pool, S0["g"], p * 2 - 2)
                nc.gpsimd.tensor_tensor(xln[:, par], x_in[:, par], mean, ALU.subtract).then_inc(S0["nstep"], 1)
                pool.wait_ge(S0["nstep"], p * 5 + 1)
                nc.gpsimd.tensor_tensor(xln[:, par], xln[:, par], rstd, ALU.mult).then_inc(S0["nstep"], 1)
                pool.wait_ge(S0["nstep"], p * 5 + 2)
                nc.gpsimd.tensor_tensor(xln[:, par], xln[:, par], w_in[:, par], ALU.mult).then_inc(S0["nstep"], 1)
                pool.wait_ge(S0["nstep"], p * 5 + 3)
                nc.gpsimd.tensor_tensor(xln[:, par], xln[:, par], b_in[:, par], ALU.add).then_inc(S0["nstep"], 1)
                pool.wait_ge(S0["nstep"], p * 5 + 4)
                pool.sem_inc(S0["seen"], 1)
                nc.gpsimd.tensor_scalar(xparts[:, par, 0], xln[:, par], 1.0, 0.0, ALU.mult, ALU.add
                                        ).then_inc(S0["nstep"], 1)
                pool.wait_ge(S0["nstep"], p * 5 + 5)
                nc.gpsimd.tensor_tensor(xparts[:, par, 1], xln[:, par], xparts[:, par, 0], ALU.subtract
                                        ).then_inc(S0["ln"], 1)

            def sum_pair(i, par):
                p = i * 2 + par
                wait(pool, S0["fin"], p * 2 + 2)
                wait(pool, S0["sstep"], p * 3)
                nc.gpsimd.tensor_tensor(sqr[:], x1[:, par], x1[:, par], ALU.mult).then_inc(S0["sstep"], 1)
                nc.gpsimd.tensor_tensor(sum1[:, 0], sum1[:, 0], x1[:, par], ALU.add).then_inc(S0["sstep"], 1)
                pool.wait_ge(S0["sstep"], p * 3 + 1)
                nc.gpsimd.tensor_tensor(sum1[:, 1], sum1[:, 1], sqr[:], ALU.add).then_inc(S0["sstep"], 1)

            def residual_pair(i, par):
                p = i * 2 + par
                wait(pool, S0["fin"], p * 2 - 2)
                pool.sem_inc(S0["seen"], 1)
                nc.gpsimd.tensor_scalar(xres[:, par], x_in[:, par], 1.0, rb0[:, 0:1], ALU.mult, ALU.add
                                        ).then_inc(S0["res"], 1)

            pool.wait_ge(stats_ready[0], 1)
            for par in range(2):
                norm_pair(0, par)
                residual_pair(0, par)
            with pool.Fori(1, NP // 2) as i:
                for par in range(2):
                    norm_pair(i, par)
                    sum_pair(i - 1, par)
                    residual_pair(i, par)
            for par in range(2):
                sum_pair(NP // 2 - 1, par)

            mean1 = mean_r[:, 0:1, :].to_broadcast([P, JT, D])
            rstd1 = rstd_r[:, 0:1, :].to_broadcast([P, JT, D])

            def norm_row(i, par):
                r = i * 2 + par
                pool.wait_ge(e_loaded[par], i * 16 + 16)
                wait(pool, S1["xt"], r - 1)
                nc.gpsimd.tensor_tensor(xn[:, par], r_in[:, par], mean1, ALU.subtract).then_inc(S1["nstep"], 1)
                pool.wait_ge(S1["nstep"], r + 1)
                nc.gpsimd.tensor_tensor(xn[:, par], xn[:, par], rstd1, ALU.mult).then_inc(S1["ln"], 1)

            def residual_row(r, par):
                wait(pool, S1["fin"], r - 1)
                nc.gpsimd.tensor_tensor(r_b[:, par], r_in[:, par], bo1_sb[:], ALU.add).then_inc(S1["res"], 1)

            pool.wait_ge(stats_ready[1], 1)
            norm_row(0, 0)
            norm_row(0, 1)
            residual_row(0, 0)
            with pool.Fori(1, NR1 // 2) as i:
                for par in range(2):
                    norm_row(i, par)
                    residual_row(i * 2 + par - 1, 1 - par)
            residual_row(NR1 - 1, 1)

        @block.tensor
        def _(pe):
            mm = nc.tensor.matmul
            PARTS = ((0, 0), (0, 1), (1, 0))

            def products(n, i, par):
                wait(pe, a_out, n - 1)
                pe.wait_ge(a_loaded[par], i * 48 + 48)
                pe.wait_ge(a_prod, n + 1)
                for half in range(CH // BANK):
                    cols = slice(half * BANK, (half + 1) * BANK)
                    for a, src in enumerate((ya, wa, ba)):
                        last = mm(psA[par][a * BW:(a + 1) * BW, half, :], wb0_sb[:], src[:, par, cols],
                                  start=True, stop=True)
                last.then_inc(a_mm, 1)

            pe.wait_ge(wb0_in, 16)
            products(0, 0, 0)
            products(1, 0, 1)
            with pe.Fori(1, NCH // 2) as i:
                for par in range(2):
                    products(i * 2 + par, i, par)

            def totals(k):
                pe.wait_ge(st_red, 2 * k + 2)
                mm(ps[:, 4, 0:2 * GROUPS], ones[:], gsum[:].rearrange("p s g -> p (s g)"),
                   start=True, stop=True).then_inc(st_mm, 1)

            pe.wait_ge(consts_set, CONSTS)
            totals(0)
            pe.wait_ge(weights_in, WEIGHTS)
            pe.wait_ge(setup_done, SETUP_OPS)
            pe.wait_ge(bias_ready, 1)

            def scores(S, r, h, nh, d, par):
                g = r * nh + h
                if h == 0:
                    pe.wait_ge(S["qe"], r + 1)
                    pe.wait_ge(S["ke"], r + 1)
                wait(pe, S["exp"], g * 2 - 2)
                m, lo = h * d // P, h * d % P
                for t in range(JT):
                    for n, (a, b) in enumerate(PARTS):
                        last = mm(psS[h % 2][:, t, :], q_sb[lo:lo + d, par, a, m, t * P:(t + 1) * P],
                                  k_sb[lo:lo + d, par, b, m, :], start=(n == 0), stop=(n == 2))
                last.then_inc(S["s"], 1)

            def turn_probs(S, g, h):
                pe.wait_ge(S["exp"], g * 2 + 2)
                wait(pe, S["pt"], g - 1)
                for t in range(JT):
                    for u in range(JT):
                        last = nc.tensor.transpose(psT[h % 2][:, u, t * P:(t + 1) * P],
                                                   p_sb[:, h % 2, t, u * P:(u + 1) * P], ident_sb[:])
                last.then_inc(S["t"], 1)

            def weigh_values(S, r, half, nh, d, par):
                pe.wait_ge(S["pt"], r * nh + (half + 1) * nh // 2)
                if half == 0:
                    pe.wait_ge(S["ve"], r + 1)
                    wait(pe, S["gate"], r)
                for u in range(JT):
                    for h in range(half * nh // 2, (half + 1) * nh // 2):
                        m, lo = h * d // P, h * d % P
                        last = mm(psO[lo:lo + d, m, :], v_sb[:, par, u, h * d:(h + 1) * d], pT_sb[:, h, u, :],
                                  start=(u == 0), stop=(u == JT - 1), skip_group_check=True)
                last.then_inc(S["av"], 1)

            def turn_sums(S, r, bank):
                pe.wait_ge(S["wide"], r + 1)
                for m in range(MT):
                    for t in range(JT):
                        last = nc.tensor.transpose(psJ[bank][:, m, t * P:(t + 1) * P],
                                                   rwide[:, t, m * P:(m + 1) * P], ident_sb[:])
                last.then_inc(S["r"], 1)

            def row0(b, k, prv, cur, nxt):
                r = b * 4 + k
                k1 = (k + 1) % 4
                xr = [xparts[:, k1 // 2, a, (k1 % 2) * W:(k1 % 2 + 1) * W] for a in range(2)]

                def project(bank, w):
                    for m in range(MT):
                        for n, (a, c) in enumerate(PARTS):
                            last = mm(psJ[bank][:, m, :], w[:, a, m * P:(m + 1) * P], xr[c],
                                      start=(n == 0), stop=(n == 2))
                    return last

                for h in range(NH0):
                    if nxt and h == 0:
                        if k1 % 2 == 0:
                            pe.wait_ge(S0["ln"], (b + (k == 3)) * 2 + k1 // 2 + 1)
                        wait(pe, S0["ve"], r + 1)
                        project(0, split0["q"]).then_inc(S0["q"], 1)
                    if nxt and h == 1:
                        wait(pe, S0["ge"], r + 1)
                        project(1, split0["k"]).then_inc(S0["k"], 1)
                    if nxt and h == 2:
                        pe.wait_ge(S0["qe"], r + 2)
                        for t in range(JT):
                            for n, (a, c) in enumerate(PARTS):
                                last = mm(psJ[0][:, t, :], xr[a][:, t * P:(t + 1) * P], split0["v"][:, c, :],
                                          start=(n == 0), stop=(n == 2))
                        last.then_inc(S0["v"], 1)
                    if nxt and h == 3:
                        pe.wait_ge(S0["ke"], r + 2)
                        project(1, split0["g"]).then_inc(S0["g"], 1)
                    if cur:
                        scores(S0, r, h, NH0, D0, k % 2)
                    if (cur and h >= 1) or (prv and h == 0):
                        turn_probs(S0, r * NH0 + h - 1, (h - 1) % 2)
                    if prv and h == 0:
                        wait(pe, S0["fin"], r - 1)
                        turn_sums(S0, r - 1, 2)
                    if prv and h == 1:
                        weigh_values(S0, r - 1, 1, NH0, D0, (k - 1) % 2)
                    if prv and h == 2:
                        pe.wait_ge(S0["gate"], r)
                        for m in range(MT):
                            last = mm(psJ[2][:, 0, :], wrep_sb[:, m, :], og_sb[:, m, :],
                                      start=(m == 0), stop=(m == MT - 1))
                        last.then_inc(S0["out"], 1)
                    if cur and h == 3:
                        weigh_values(S0, r, 0, NH0, D0, k % 2)

            each_row(pe, H, 4, row0)

            totals(1)

            def row1(b, k, prv, cur, nxt):
                r = b * 2 + k
                par = (k + 1) % 2

                def project(bank, w):
                    for m in range(MT):
                        for c in range(MT):
                            for n, (a, e) in enumerate(PARTS):
                                last = mm(psJ[bank][:, m, :], w[:, a, c, m * P:(m + 1) * P], xnT[:, e, c, :],
                                          start=(c + n == 0), stop=(c == MT - 1 and n == 2))
                    return last

                for h in range(NH1):
                    if nxt and h == 0:
                        pe.wait_ge(S1["ln"], r + 2)
                        wait(pe, S1["ge"], r + 1)
                        for m in range(MT):
                            for t in range(JT):
                                last = nc.tensor.transpose(psJ[0][:, m, t * P:(t + 1) * P],
                                                           xn[:, par, t, m * P:(m + 1) * P], ident_sb[:])
                        last.then_inc(S1["xt"], 1)
                    if nxt and h == 2:
                        pe.wait_ge(S1["xte"], r + 2)
                        wait(pe, S1["ve"], r + 1)
                        project(1, split1["q"]).then_inc(S1["q"], 1)
                    if nxt and h == 3:
                        project(0, split1["k"]).then_inc(S1["k"], 1)
                    if nxt and h == 4:
                        pe.wait_ge(S1["qe"], r + 2)
                        for t in range(JT):
                            for c in range(MT):
                                for n, (a, e) in enumerate(PARTS):
                                    last = mm(psJ[1][:, t, :], xnT[:, a, c, t * P:(t + 1) * P],
                                              split1["v"][:, e, c, :],
                                              start=(c + n == 0), stop=(c == MT - 1 and n == 2))
                        last.then_inc(S1["v"], 1)
                    if nxt and h == 5:
                        pe.wait_ge(S1["ke"], r + 2)
                        project(0, split1["g"]).then_inc(S1["g"], 1)
                    if prv and h >= 6:
                        pe.wait_ge(S1["gate"], r)
                        t = h - 6
                        for m in range(MT):
                            last = mm(psJ[2][:, t, :], og_sb[:, m, t * P:(t + 1) * P], wo1_sb[:, m, :],
                                      start=(m == 0), stop=(m == MT - 1))
                        if t == JT - 1:
                            last.then_inc(S1["out"], 1)
                    if cur:
                        scores(S1, r, h, NH1, D1, k % 2)
                    if (cur and h >= 1) or (prv and h == 0):
                        turn_probs(S1, r * NH1 + h - 1, (h - 1) % 2)
                    if prv and h == 1:
                        wait(pe, S1["fin"], r - 1)
                        turn_sums(S1, r - 1, 2)
                        weigh_values(S1, r - 1, 1, NH1, D1, (k - 1) % 2)
                    if cur and h == 6:
                        weigh_values(S1, r, 0, NH1, D1, k % 2)

            pe.wait_ge(stats_ready[1], 1)
            each_row(pe, NR1, 2, row1)

        @block.scalar
        def _(act):
            def chunk(n, i, par):
                act.wait_ge(a_loaded[par], i * 48 + 48)
                wait(act, a_sum, n * 2)
                nc.scalar.activation(sq[:, par], xa[:, par], ACT.Square).then_inc(a_sq, 1)
                act.wait_ge(a_mm, n + 1)
                wait(act, a_stored[par], i * 48)
                nc.scalar.activation(prod[:, par].rearrange("p (h n) -> p h n", n=BANK), psA[par],
                                     ACT.Copy).then_inc(a_out, 1)

            chunk(0, 0, 0)
            chunk(1, 0, 1)
            with act.Fori(1, NCH // 2) as i:
                for par in range(2):
                    chunk(i * 2 + par, i, par)

            def sqrt_of(col, n, count):
                act.wait_ge(st_var, count)
                nc.scalar.activation(st[:, col, 0:n], st[:, col - 1, 0:n], ACT.Sqrt).then_inc(st_sqrt, 1)

            sqrt_of(1, GROUPS, 1)
            sqrt_of(5, 1, 2)
            act.wait_ge(setup_done, SETUP_OPS)

            def exponentials(S, r, h, nh, par):
                act.wait_ge(S["max"], r * nh + h + 1)
                for t in range(JT):
                    nc.scalar.activation(p_sb[:, h % 2, t, :], psS[h % 2][:, t, :], ACT.Exp,
                                         bias=nmax[:, par, 2 * h + t:2 * h + t + 1], scale=-1.0,
                                         accum_out=rsum[:, par, 2 * h + t:2 * h + t + 1]).then_inc(S["exp"], 1)

            def copy_turned(S, g, h):
                act.wait_ge(S["t"], g + 1)
                nc.scalar.activation(pT_sb[:, h], psT[h % 2], ACT.Copy).then_inc(S["pt"], 1)

            def gates(S, r, bank, par, half_bias):
                act.wait_ge(S["g"], r + 1)
                wait(act, S["gr"], r - 1)
                for m in range(MT):
                    last = nc.scalar.activation(th_sb[:, par, m, :], psJ[bank][:, m, :], ACT.Tanh,
                                                bias=half_bias[:, m:m + 1], scale=0.5)
                last.then_inc(S["ge"], 1)

            def row0(b, k, prv, cur, nxt):
                r = b * 4 + k
                par = (k + 1) % 2
                for h in range(NH0):
                    if (cur and h >= 2) or (prv and h < 2):
                        copy_turned(S0, r * NH0 + h - 2, (h - 2) % NH0)
                    if nxt and h == 0:
                        act.wait_ge(S0["q"], r + 2)
                        nc.scalar.activation(q_sb[:, par, 0], psJ[0], ACT.Copy, scale=-SCALE0).then_inc(S0["qh"], 1)
                    if nxt and h == 1:
                        act.wait_ge(S0["k"], r + 2)
                        nc.scalar.activation(k_sb[:, par, 0], psJ[1], ACT.Copy).then_inc(S0["kh"], 1)
                    if nxt and h == 3:
                        gates(S0, r + 1, 1, par, gb0)
                    if cur:
                        exponentials(S0, r, h, NH0, k % 2)

            each_row(act, H, 4, row0)

            sqrt_of(1, GROUPS, 3)

            def row1(b, k, prv, cur, nxt):
                r = b * 2 + k
                par = (k + 1) % 2
                for h in range(NH1):
                    if (cur and h >= 2) or (prv and h < 2):
                        copy_turned(S1, r * NH1 + h - 2, (h - 2) % NH1)
                    if nxt and h == 0:
                        act.wait_ge(S1["xt"], r + 2)
                        nc.scalar.activation(xnT[:, 0], psJ[0], ACT.Copy).then_inc(S1["xh"], 1)
                    if nxt and h == 2:
                        act.wait_ge(S1["q"], r + 2)
                        nc.scalar.activation(q_sb[:, par, 0], psJ[1], ACT.Copy, scale=-SCALE1).then_inc(S1["qh"], 1)
                    if nxt and h == 3:
                        act.wait_ge(S1["k"], r + 2)
                        nc.scalar.activation(k_sb[:, par, 0], psJ[0], ACT.Copy).then_inc(S1["kh"], 1)
                    if nxt and h == 5:
                        gates(S1, r + 1, 0, par, gb1)
                    if cur:
                        exponentials(S1, r, h, NH1, k % 2)

            each_row(act, NR1, 2, row1)

        @block.vector
        def _(dve):
            nc.vector.memset(sum0[:], 0.0).then_inc(a_sum, 2)

            def chunk(n, i, par):
                dve.wait_ge(a_loaded[par], i * 48 + 48)
                wait(dve, a_mm, n - 1)
                nc.vector.tensor_tensor(ya[:, par], xa[:, par], wa[:, par], ALU.mult).then_inc(a_prod, 1)
                dve.wait_ge(a_sum, n * 2 + 2)
                nc.vector.tensor_tensor(sum0[:, 0], sum0[:, 0], xa[:, par], ALU.add).then_inc(a_sum, 1)
                dve.wait_ge(a_sq, n + 1)
                nc.vector.tensor_tensor(sum0[:, 1], sum0[:, 1], sq[:, par], ALU.add).then_inc(a_sum, 1)

            chunk(0, 0, 0)
            chunk(1, 0, 1)
            with dve.Fori(1, NCH // 2) as i:
                for par in range(2):
                    chunk(i * 2 + par, i, par)

            done = [0]

            def then(instruction):
                done[0] += 1
                instruction.then_inc(st_step, 1)
                dve.wait_ge(st_step, done[0])

            v = nc.vector
            mean, ex2, var = st[:, 6, :], st[:, 7, :], st[:, 0, :]

            def inverse_root(col, n, to):
                a, root, t = st[:, col, 0:n], st[:, col + 1, 0:n], st[:, col + 2, 0:n]
                then(v.reciprocal(to, root))
                then(v.tensor_tensor(t, to, to, ALU.mult))
                then(v.tensor_tensor(t, t, a, ALU.mult))
                then(v.tensor_scalar(t, t, -0.5, 1.5, ALU.mult, ALU.add))
                then(v.tensor_tensor(to, to, t, ALU.mult))

            def group_stats(sums, rows, k):
                for s in range(2):
                    v.tensor_reduce(gsum[:, s, :], sums[:, s, :].rearrange("p (r g e) -> p g r e", r=rows, e=GS),
                                    AX.XY, ALU.add).then_inc(st_red, 1)
                dve.wait_ge(st_mm, k + 1)
                then(v.tensor_scalar(st[:, 6:8, :], ps[:, 4, 0:2 * GROUPS].rearrange("p (s g) -> p s g", s=2),
                                     1.0 / COUNT, None, ALU.mult))
                then(v.tensor_tensor(st[:, 3, :], mean, mean, ALU.mult))
                then(v.tensor_tensor(st[:, 3, :], ex2, st[:, 3, :], ALU.subtract))
                then(v.tensor_scalar(st[:, 3, :], st[:, 3, :], 0.0, None, ALU.max))

            dve.wait_ge(a_sum, NCH * 2 + 2)
            group_stats(sum0, QR, 0)
            v.tensor_scalar(var, st[:, 3, :], EPS_NORM, None, ALU.add).then_inc(st_var, 1)
            dve.wait_ge(st_var, 1)
            dve.wait_ge(st_sqrt, 1)
            gr = gtot[:, 0, :]
            inverse_root(0, GROUPS, gr)
            then(v.tensor_tensor(st[:, 2, :], gr, gr, ALU.mult))
            then(v.tensor_tensor(st[:, 2, :], st[:, 2, :], st[:, 3, :], ALU.mult))
            then(v.tensor_reduce(tall[:, 0:1], st[:, 2, :], AX.X, ALU.add))
            v.tensor_scalar(st[:, 4, 0:1], tall[:, 0:1], 1.0 / GROUPS, EPS_NORM, ALU.mult, ALU.add
                            ).then_inc(st_var, 1)
            dve.wait_ge(st_var, 2)
            dve.wait_ge(st_sqrt, 2)
            inverse_root_1 = tall[:, 1:2]
            then(v.reciprocal(inverse_root_1, st[:, 5, 0:1]))
            then(v.tensor_tensor(tall[:, 2:3], inverse_root_1, inverse_root_1, ALU.mult))
            then(v.tensor_tensor(tall[:, 2:3], tall[:, 2:3], st[:, 4, 0:1], ALU.mult))
            then(v.tensor_scalar(tall[:, 2:3], tall[:, 2:3], -0.5, 1.5, ALU.mult, ALU.add))
            then(v.tensor_tensor(inverse_root_1, inverse_root_1, tall[:, 2:3], ALU.mult))
            then(v.tensor_scalar(gr, gr, inverse_root_1, None, ALU.mult))

            def spread(r):
                for dst, src in ((mean_r, mean), (rstd_r, gr)):
                    then(v.tensor_copy(dst[:, r, :].rearrange("p (g e) -> p g e", e=GS),
                                       src.unsqueeze(2).to_broadcast([P, GROUPS, GS])))

            for r in range(PR):
                spread(r)
            dve.wait_ge(parts_in, 16 * 3 * JT)
            parts = [parts_sb[:, a].rearrange("p h t k -> p (h t) k") for a in range(3)]
            wide = [P, NH0 * JT, W]
            then(v.tensor_tensor(parts[1], parts[1], mean_r[:, 0:1, :].to_broadcast(wide), ALU.mult))
            then(v.tensor_tensor(parts[0], parts[0], parts[1], ALU.subtract))
            then(v.tensor_tensor(parts[0], parts[0], rstd_r[:, 0:1, :].to_broadcast(wide), ALU.mult))
            flat = [parts_sb[:, a].rearrange("p h t k -> p (h t k)") for a in (0, 2)]
            v.scalar_tensor_tensor(out=nbias0[:].rearrange("p h t k -> p (h t k)"), in0=flat[0], scalar=-1.0,
                                   in1=flat[1], op0=ALU.mult, op1=ALU.subtract).then_inc(bias_ready, 1)
            dve.wait_ge(bias_ready, 1)
            v.tensor_copy(tall[:, 3:4], tall[:, 1:2]).then_inc(stats_ready[0], 1)
            dve.wait_ge(setup_done, SETUP_OPS)
            dve.wait_ge(consts_set, CONSTS)

            def bias_and_max(S, r, h, nh, par, nbias):
                dve.wait_ge(S["s"], r * nh + h + 1)
                dve.sem_inc(S["seen"], 1)
                for t in range(JT):
                    last = v.tensor_tensor_reduce(psS[h % 2][:, t, :], psS[h % 2][:, t, :], nbias[:, h, t, :], 1.0, BIG,
                                           ALU.add, ALU.min, nmax[:, par, 2 * h + t:2 * h + t + 1])
                last.then_inc(S["max"], 1)

            def invert_sums(S, r, nh, par):
                dve.wait_ge(S["exp"], (r + 1) * nh * 2)
                v.reciprocal(rinv[:, 0:nh * JT], rsum[:, par, 0:nh * JT]).then_inc(S["den"], 1)
                dve.wait_ge(S["den"], r + 1)
                v.tensor_copy(rwide[:].rearrange("p t (h e) -> p t h e", h=nh),
                              rinv[:, 0:nh * JT].rearrange("p (h t) -> p t h", t=JT).unsqueeze(3)
                              .to_broadcast([P, JT, nh, MT * P // nh])).then_inc(S["wide"], 1)

            def gates_over_sums(S, r, bank, par):
                dve.wait_ge(S["r"], r + 1)
                dve.wait_ge(S["ge"], r + 1)
                v.scalar_tensor_tensor(out=gr_sb[:].rearrange("p m j -> p (m j)"),
                                       in0=th_sb[:, par].rearrange("p m j -> p (m j)"), scalar=1.0,
                                       in1=psJ[bank].rearrange("p m j -> p (m j)"),
                                       op0=ALU.add, op1=ALU.mult).then_inc(S["gr"], 1)

            def gate_outputs(S, r):
                dve.wait_ge(S["av"], (r + 1) * 2)
                dve.wait_ge(S["gr"], r + 1)
                v.tensor_tensor(og_sb[:], psO, gr_sb[:], ALU.mult).then_inc(S["gate"], 1)

            def copy_values(S, r, bank, par):
                dve.wait_ge(S["v"], r + 1)
                v.tensor_copy(v_sb[:, par], psJ[bank]).then_inc(S["ve"], 1)

            def low_part(dst, high, src, scale, done, sem_low, count):
                dve.wait_ge(done, count)
                v.scalar_tensor_tensor(out=dst.rearrange("p m j -> p (m j)"), in0=src.rearrange("p m j -> p (m j)"),
                                       scalar=scale, in1=high.rearrange("p m j -> p (m j)"),
                                       op0=ALU.mult, op1=ALU.subtract).then_inc(sem_low, 1)

            def row0(b, k, prv, cur, nxt):
                r = b * 4 + k
                par = (k + 1) % 2
                for h in range(NH0):
                    if prv and h == 0:
                        invert_sums(S0, r - 1, NH0, par)
                    if prv and h == 2:
                        gate_outputs(S0, r - 1)
                    if prv and h == 3:
                        kp = (k - 1) % 4
                        pair, half = kp // 2, kp % 2
                        dve.wait_ge(S0["out"], r)
                        if half == 0:
                            i = b - (k == 0)
                            dve.wait_ge(S0["res"], i * 2 + pair + 1)
                            wait(dve, S0["sstep"], (i * 2 + pair - 1) * 3)
                            wait(dve, c_stored[pair], i * 16)
                        v.tensor_tensor(x1[:, pair, half * W:(half + 1) * W], psJ[2][:, 0, :],
                                        xres[:, pair, half * W:(half + 1) * W], ALU.add).then_inc(S0["fin"], 1)
                    if cur:
                        bias_and_max(S0, r, h, NH0, k % 2, nbias0)
                    if nxt and h == 0:
                        low_part(q_sb[:, par, 1], q_sb[:, par, 0], psJ[0], -SCALE0, S0["qh"], S0["qe"], r + 2)
                    if nxt and h == 1:
                        low_part(k_sb[:, par, 1], k_sb[:, par, 0], psJ[1], 1.0, S0["kh"], S0["ke"], r + 2)
                    if prv and h == 1:
                        gates_over_sums(S0, r - 1, 2, par)
                    if nxt and h == 2:
                        copy_values(S0, r + 1, 0, par)

            each_row(dve, H, 4, row0)

            dve.wait_ge(S0["sstep"], NP * 3)
            group_stats(sum1, PR, 1)
            v.tensor_scalar(var, st[:, 3, :], EPS_NORM, None, ALU.add).then_inc(st_var, 1)
            dve.wait_ge(st_var, 3)
            dve.wait_ge(st_sqrt, 3)
            inverse_root(0, GROUPS, gr)
            spread(0)
            v.tensor_copy(tall[:, 3:4], gr[:, 0:1]).then_inc(stats_ready[1], 1)

            def row1(b, k, prv, cur, nxt):
                r = b * 2 + k
                par = (k + 1) % 2
                for h in range(NH1):
                    if prv and h == 1:
                        invert_sums(S1, r - 1, NH1, par)
                    if prv and h == 2:
                        gates_over_sums(S1, r - 1, 2, par)
                    if prv and h == 3:
                        gate_outputs(S1, r - 1)
                    if prv and h == 7:
                        dve.wait_ge(S1["out"], r)
                        dve.wait_ge(S1["res"], r)
                        wait(dve, e_stored[par], (b - (k == 0)) * 16)
                        v.tensor_tensor(y_sb[:, par], psJ[2], r_b[:, par], ALU.add).then_inc(S1["fin"], 1)
                    if cur:
                        bias_and_max(S1, r, h, NH1, k % 2, nbias1)
                    if nxt and h == 0:
                        low_part(xnT[:, 1], xnT[:, 0], psJ[0], 1.0, S1["xh"], S1["xte"], r + 2)
                    if nxt and h == 2:
                        low_part(q_sb[:, par, 1], q_sb[:, par, 0], psJ[1], -SCALE1, S1["qh"], S1["qe"], r + 2)
                    if nxt and h == 3:
                        low_part(k_sb[:, par, 1], k_sb[:, par, 0], psJ[0], 1.0, S1["kh"], S1["ke"], r + 2)
                    if nxt and h == 4:
                        copy_values(S1, r + 1, 1, par)

            each_row(dve, NR1, 2, row1)


def kernel(**inputs):
    import numpy as _np
    import concourse.bacc as _bacc
    from concourse import mybir as _mybir
    from concourse.bass_utils import run_bass_kernel_spmd as _run

    def a(name):
        return _np.asarray(inputs[name])

    C, H, W = a("x").shape[1:]
    nh0 = a("L0_conv_wb").shape[0]
    hc0 = a("L0_conv_wq").shape[0]
    given = {
        "x": a("x")[0], "ln_w": a("L0_conv_ln_w"), "ln_b": a("L0_conv_ln_b"),
        "wq0": a("L0_conv_wq").T, "wk0": a("L0_conv_wk").T, "wv0": a("L0_conv_wv").T, "wg0": a("L0_conv_wg_w").T,
        "wb0": a("L0_conv_wb").T, "wg0_b": a("L0_conv_wg_b").reshape(-1, 128).T,
        "wrep": a("L0_conv_wrep_w").reshape(C, hc0 // nh0, nh0).transpose(2, 1, 0).reshape(hc0, C),
        "wrep_b": a("L0_conv_wrep_b").reshape(C, 1),
        "pair_bias1": a("L1_conv_nonbatched_bias")[0],
        "wq1": a("L1_conv_Wq").T, "wk1": a("L1_conv_Wk").T, "wv1": a("L1_conv_Wv").T, "wg1": a("L1_conv_Wg").T,
        "wg1_b": a("L1_conv_gating_bias").reshape(-1, 128).T,
        "wo1": a("L1_conv_Wo").T, "bo1": a("L1_conv_bo"),
        "ident": _np.eye(128, dtype=_np.float32),
    }
    nc = _bacc.Bacc("TRN2", target_bir_lowering=False, num_devices=1)
    arrays, args = {}, []
    for name, array in given.items():
        array = _np.ascontiguousarray(array)
        arrays[f"in_{name}_dram"] = array
        args.append(nc.dram_tensor(f"in_{name}_dram", array.shape, _mybir.dt.from_np(array.dtype),
                                   kind="ExternalInput").ap())
    args.append(nc.dram_tensor("out_0_dram", (C, H, W), _mybir.dt.float32, kind="ExternalOutput").ap())
    two_layers(nc, *args)
    r = _run(nc, [arrays], core_ids=[0])
    return r.results[0]["out_0_dram"].reshape(1, C, H, W)
```

```python
from contextlib import ExitStack

import concourse.bass as bass
from concourse import mybir

ALU = mybir.AluOpType
ACT = mybir.ActivationFunctionType
AX = mybir.AxisListType
F32 = mybir.dt.float32
F16 = mybir.dt.float16

P = 128
BANK = 512
BIG = 3.0e38
GROUPS = 32
EPS_NORM = 1e-5


def wait(eng, sem, value):
    if isinstance(value, int) and value <= 0:
        return
    eng.wait_ge(sem, value)


def each_row(eng, rows, blk, row):
    n = rows // blk
    row(-1, blk - 1, False, False, True)
    for k in range(blk):
        row(0, k, k > 0, True, True)
    with eng.Fori(1, n - 1) as b:
        for k in range(blk):
            row(b, k, True, True, True)
    for k in range(blk):
        row(n - 1, k, True, True, k < blk - 1)
    row(n, 0, True, False, False)


BY_DVE = {4: (), 8: (4, 5, 6)}


def copied(eng, S, r, h, nh):
    mine = [n for n in range(nh) if (n in BY_DVE[nh]) == (h in BY_DVE[nh])]
    wait(eng, S["ptv" if h in BY_DVE[nh] else "pt"], r * len(mine) + mine.index(h) + 1)


def two_layers(nc, x, ln_w, ln_b, wq0, wk0, wv0, wg0, wb0, wg0_b, wrep, wrep_b,
               pair_bias1, wq1, wk1, wv1, wg1, wg1_b, wo1, bo1, ident, out):
    C, H, W = x.shape
    JT = W // P
    NH0 = wb0.shape[1]
    D0 = wq0.shape[1] // NH0
    NH1 = pair_bias1.shape[0]
    D1 = wq1.shape[1] // NH1
    D = W
    MT = wq0.shape[1] // P
    GS = W // GROUPS
    COUNT = float(C * H * GS)
    SCALE0 = float(D0) ** -0.5
    SCALE1 = float(D1) ** -0.5
    QR = 4
    CH = QR * W
    NCH = H // QR
    PR = 2
    PW = PR * W
    NP = H // PR
    NR1 = C
    BW = 32

    with ExitStack() as ctx:
        def sb(name, shape, dt=F32):
            return ctx.enter_context(nc.sbuf_tensor(name, shape, dt))

        def sem(name):
            return ctx.enter_context(nc.semaphore(name))

        ps = ctx.enter_context(nc.psum_tensor("ps", [P, 8, BANK], F32))
        psS = [ps[:, b, :].rearrange("p (t k) -> p t k", t=JT) for b in (0, 1)]
        psT = [ps[:, b, :].rearrange("p (t j) -> p t j", t=JT) for b in (2, 3)]
        psJ = [ps[:, b, :].rearrange("p (t j) -> p t j", t=2) for b in (4, 5, 6)]
        psO = ps[:, 7, :].rearrange("p (m j) -> p m j", m=2)
        psA = [ps[0:3 * BW, b:b + 2, :] for b in (0, 2)]

        ident_sb = sb("ident_sb", [P, P])
        ones = sb("ones", [P, P])
        wq0_sb, wk0_sb = (sb(n, [P, MT * P]) for n in ("wq0_sb", "wk0_sb"))
        wb0_sb = sb("wb0_sb", [P, BW])
        gb0 = sb("gb0", [P, MT])
        gb1 = sb("gb1", [P, MT])
        rb0 = sb("rb0", [P, 1])
        split0 = {n: sb(f"{n}0_parts", [P, 2, MT * P], F16) for n in "qkvg"}
        split1 = {n: sb(f"{n}1_parts", [P, 2, MT, D], F16) for n in "qkvg"}
        wrep_sb = sb("wrep_sb", [P, MT, C])
        wo1_parts = sb("wo1_parts", [P, 2, MT, D], F16)
        bo1_sb = sb("bo1_sb", [P, JT, D])
        nbias0 = sb("nbias0", [P, NH0, JT, W])
        nbias1 = sb("nbias1", [P, NH1, JT, W])

        abuf = sb("abuf", [P, 3, 2, CH])
        ya, sq = (sb(n, [P, 2, CH]) for n in ("ya", "sq"))
        prod = sb("prod", [3 * BW, 2, CH])
        sum0 = sb("sum0", [P, 2, CH])
        bias_parts = nc.dram_tensor("bias_parts", [3, NH0, H, W], F32, kind="Internal").ap()

        gsum = sb("gsum", [P, 2, GROUPS])
        gtot = sb("gtot", [P, 2, GROUPS])
        st = sb("st", [P, 8, GROUPS])
        tall = sb("tall", [P, 4])
        mean_r, rstd_r = sb("mean_r", [P, PR, W]), sb("rstd_r", [P, PR, W])
        parts_sb = abuf[:].rearrange("p a n (m t k) -> p a (n m) t k", t=JT, k=W)

        x_in, w_in, b_in, xln, xres, x1 = (
            sb(n, [P, 2, PW]) for n in ("x_in", "w_in", "b_in", "xln", "xres", "x1"))
        wq1_sb, wk1_sb, wv1_sb, wg1_sb = (buf[:, n].rearrange("p (t d) -> p t d", t=MT)
                                          for buf in (w_in, b_in) for n in range(2))
        wv0_sb, wg0_sb = (xln[:, 0, n * MT * P:(n + 1) * MT * P] for n in range(2))
        wo1_sb = xln[:, 1].rearrange("p (t d) -> p t d", t=MT)
        sqr = sb("sqr", [P, PW])
        sum1 = sb("sum1", [P, 2, PW])
        xparts = sb("xparts", [P, 2, 2, PW], F16)
        qk_sb = sb("qk_sb", [P, 2, 4, MT, W], F16)
        HH0, HH1 = P // D0, P // D1
        stacked = sb("stacked", [P, 2, HH1, 2, MT, W], F16)
        stacked1 = stacked[:]
        stacked0 = stacked1.rearrange("p b h s m w -> p b (h s) m w")[:, :, 0:3 * HH0].rearrange(
            "p b (h s) m w -> p b h s m w", s=3)
        th_sb = sb("th_sb", [P, 2, MT, W])
        v_sb = sb("v_sb", [P, 2, JT, MT * P])
        p_sb = sb("p_sb", [P, 4, JT, W])
        pT_sb = sb("pT_sb", [P, NH1, JT, W])
        nmax = sb("nmax", [P, 2, 2 * NH1])
        rsum = sb("rsum", [P, 2, 2 * NH1])
        rinv = sb("rinv", [P, 2 * NH1])
        rwide = sb("rwide", [P, JT, MT * P])
        gr_sb = sb("gr_sb", [P, MT, W])
        og_sb = sb("og_sb", [P, MT, W])
        og_parts = sb("og_parts", [P, 2, MT, W], F16)

        late = [pT_sb[:].rearrange("p (a n h) t k -> p a n (h t k)", a=2, n=2)[:, a] for a in range(2)]
        late.append(p_sb[:].rearrange("p (n h) t k -> p n (h t k)", n=2))
        xa, wa, ba = ([abuf[:, a, 0], abuf[:, a, 1], late[a][:, 0], late[a][:, 1]] for a in range(3))

        r_in, xn, r_b, y_sb = (buf[:, n].rearrange("p (b t d) -> p b t d", b=2, t=JT)
                               for buf in (ya, sq) for n in range(2))
        xnT = sb("xnT", [P, 2, MT, W], F16)

        x1_dram = nc.dram_tensor("x1_dram", [C, H, W], F32, kind="Internal").ap()

        sp_seen = sem("sp_seen")
        wb0_in = sem("wb0_in")
        weights_in = sem("weights_in")
        consts_set = sem("consts_set")
        setup_done = sem("setup_done")
        split_step = sem("split_step")
        a_loaded = [sem(f"a_loaded{k}") for k in range(4)]
        a_prod, a_sum, a_sq = sem("a_prod"), sem("a_sum"), sem("a_sq")
        a_mm, a_out = sem("a_mm"), sem("a_out")
        a_stored = [sem("a_stored0"), sem("a_stored1")]
        st_step, st_red, st_mm = sem("st_step"), sem("st_red"), sem("st_mm")
        st_var, st_sqrt = sem("st_var"), sem("st_sqrt")
        parts_in, bias_ready = sem("parts_in"), sem("bias_ready")
        stats_ready = [sem("stats_ready0"), sem("stats_ready1")]

        def layer_sems(n):
            names = ("s", "t", "av", "q", "k", "v", "g", "r", "out", "max", "exp", "qh", "qe", "kh", "ke", "ve", "ge",
                     "pt", "ptv", "den", "wide", "gr", "gate", "oh", "oe", "fin", "xh", "nstep", "ln", "sstep", "res", "xt", "xte", "seen")
            return {k: sem(f"l{n}_{k}") for k in names}

        S0, S1 = layer_sems(0), layer_sems(1)
        l0_stacked = [sem(f"l0_stacked{par}") for par in range(2)]
        l1_stacked = [[sem(f"l1_stacked{par}_{hh}") for hh in range(P // D1)] for par in range(2)]
        c_loaded = [sem("c_loaded0"), sem("c_loaded1")]
        c_stored = [sem("c_stored0"), sem("c_stored1")]
        e_loaded = [sem("e_loaded0"), sem("e_loaded1")]
        e_stored = [sem("e_stored0"), sem("e_stored1")]

        def by_pair(a):
            return a.rearrange("c (p r) j -> p c (r j)", r=PR)

        def by_chunk(a):
            return a.rearrange("c (n r) j -> n c (r j)", r=QR)

        x_c, w_c, b_c = by_chunk(x), by_chunk(ln_w), by_chunk(ln_b)
        x_p, w_p, b_p, x1_p = by_pair(x), by_pair(ln_w), by_pair(ln_b), by_pair(x1_dram)
        parts_c = bias_parts.rearrange("a h (n r) j -> n a h (r j)", r=QR)
        x1_l = x1_dram.rearrange("b (t l) d -> b l t d", t=JT)
        out_l = out.rearrange("b (t l) d -> b l t d", t=JT)

        weight_loads = [
            (ident_sb[:], ident), (wq0_sb[:], wq0), (wk0_sb[:], wk0), (wv0_sb[:], wv0), (wg0_sb[:], wg0),
            (wrep_sb[:], wrep.rearrange("(t p) o -> p t o", p=P)),
            (gb0[:], wg0_b), (gb1[:], wg1_b), (rb0[:], wrep_b),
            (wq1_sb[:], wq1.rearrange("(t p) o -> p t o", p=P)),
            (wk1_sb[:], wk1.rearrange("(t p) o -> p t o", p=P)),
            (wv1_sb[:], wv1.rearrange("(t p) o -> p t o", p=P)),
            (wg1_sb[:], wg1.rearrange("(t p) o -> p t o", p=P)),
            (wo1_sb[:], wo1.rearrange("(t p) o -> p t o", p=P)),
        ]
        weight_loads += [(bo1_sb[:, t, :], bo1.partition_broadcast(P)) for t in range(JT)]
        weight_loads += [(nbias1[:, h], pair_bias1[h].rearrange("(t p) k -> p t k", p=P)) for h in range(NH1)]
        WEIGHTS = 16 * len(weight_loads)
        CONSTS = 3
        SETUP_OPS = 4

        block = ctx.enter_context(nc.Block())

        @block.sync
        def _(sp):
            sp.wait_ge(consts_set, 1)
            sp.dma_start(wb0_sb[:, 0:NH0], wb0).then_inc(wb0_in, 16)

            def load_chunk(n, k):
                wait(sp, a_mm, n - 3)
                sp.sem_inc(sp_seen, 1)
                wait(sp, a_sum, n * 2 - 4)
                sp.dma_start(xa[k], x_c[n]).then_inc(a_loaded[k], 16)
                sp.dma_start(wa[k], w_c[n]).then_inc(a_loaded[k], 16)
                sp.dma_start(ba[k], b_c[n]).then_inc(a_loaded[k], 16)

            def store_products(n, par):
                wait(sp, a_out, n + 1)
                for a in range(3):
                    sp.dma_start(parts_c[n, a], prod[a * BW:a * BW + NH0, par]).then_inc(a_stored[par], 16)

            for k in range(4):
                load_chunk(k, k)
            for dst, src in weight_loads:
                sp.dma_start(dst, src).then_inc(weights_in, 16)
            for k in range(2):
                store_products(k, k)
            for k in range(2):
                load_chunk(4 + k, k)
                store_products(2 + k, k)
            with sp.Fori(1, NCH // 4 - 1) as i:
                for k in range(4):
                    load_chunk(i * 4 + k + 2, (k + 2) % 4)
                    store_products(i * 4 + k, k % 2)
            for k in range(2):
                load_chunk(NCH - 2 + k, 2 + k)
                store_products(NCH - 4 + k, k)
            for k in range(2):
                store_products(NCH - 2 + k, k)

            for par in range(2):
                sp.wait_ge(a_stored[par], 48 * (NCH // 2))
            sp.wait_ge(a_sum, NCH * 2 + 2)
            sp.wait_ge(a_mm, NCH)
            for a in range(3):
                for t in range(JT):
                    sp.dma_start(parts_sb[:, a, :, t, :],
                                 bias_parts[a, :, t * P:(t + 1) * P, :].rearrange("h p j -> p h j")
                                 ).then_inc(parts_in, 16)

            def load_pair(p, par):
                wait(sp, S0["res"], p - 1)
                sp.dma_start(x_in[:, par], x_p[p]).then_inc(c_loaded[par], 16)
                sp.dma_start(w_in[:, par], w_p[p]).then_inc(c_loaded[par], 16)
                sp.dma_start(b_in[:, par], b_p[p]).then_inc(c_loaded[par], 16)

            def store_pair(p, par):
                wait(sp, S0["fin"], p * 2 + 2)
                sp.dma_start(x1_p[p], x1[:, par]).then_inc(c_stored[par], 16)

            def row0(b, k, prv, cur, nxt):
                r = b * 4 + k
                if cur and k % 2 == 0 and not (isinstance(b, int) and b * 2 + k // 2 + 2 >= NP):
                    load_pair(b * 2 + k // 2 + 2, k // 2)
                if nxt:
                    par = (k + 1) % 2
                    sp.wait_ge(S0["qe"], r + 2)
                    for hh in range(HH0):
                        for a in range(2):
                            sp.dma_start(stacked0[a * D0:(a + 1) * D0, par, hh, 0],
                                         qk_sb[hh * D0:(hh + 1) * D0, par, a]).then_inc(l0_stacked[par], 16)
                    sp.wait_ge(S0["ke"], r + 2)
                    for hh in range(HH0):
                        for a in range(2):
                            sp.dma_start(stacked0[a * D0:(a + 1) * D0, par, hh, 1:3],
                                         qk_sb[hh * D0:(hh + 1) * D0, par, 2:4]).then_inc(l0_stacked[par], 16)
                if prv and cur and k % 2 == 1 and not (isinstance(b, int) and b * 2 + k // 2 < 1):
                    store_pair(b * 2 + k // 2 - 1, (k // 2 + 1) % 2)

            sp.wait_ge(setup_done, SETUP_OPS)
            load_pair(0, 0)
            load_pair(1, 1)
            each_row(sp, H, 4, row0)
            store_pair(NP - 1, 1)

            for par in range(2):
                sp.wait_ge(c_stored[par], 16 * (NP // 2))

            def load_row(r, par):
                wait(sp, S1["res"], r - 1)
                sp.dma_start(r_in[:, par], x1_l[r]).then_inc(e_loaded[par], 16)

            def store_row(r, par):
                wait(sp, S1["fin"], r + 1)
                sp.dma_start(out_l[r], y_sb[:, par]).then_inc(e_stored[par], 16)

            def row1(b, k, prv, cur, nxt):
                r = b * 2 + k
                if not (isinstance(r, int) and r < 2):
                    store_row(r - 2, k)
                if cur and not (isinstance(r, int) and r + 2 >= NR1):
                    load_row(r + 2, k)
                if nxt:
                    par = (k + 1) % 2
                    sp.wait_ge(S1["ke"], r + 2)
                    for hh in range(HH1):
                        for n in range(HH1):
                            q, k_ = n // 2, 2 + n % 2
                            sp.dma_start(stacked1[n * D1:(n + 1) * D1, par, hh],
                                         qk_sb[hh * D1:(hh + 1) * D1, par, q:k_ + 1:k_ - q]
                                         ).then_inc(l1_stacked[par][hh], 16)

            load_row(0, 0)
            load_row(1, 1)
            each_row(sp, NR1, 2, row1)
            store_row(NR1 - 1, 1)
            for par in range(2):
                sp.wait_ge(e_stored[par], 16 * (NR1 // 2))

        @block.gpsimd
        def _(pool):
            nc.gpsimd.memset(wb0_sb[:], 0.0).then_inc(consts_set, 1)
            nc.gpsimd.memset(ones[:], 1.0).then_inc(consts_set, 1)
            nc.gpsimd.memset(sum1[:], 0.0).then_inc(consts_set, 1)
            pool.wait_ge(weights_in, WEIGHTS)
            nc.gpsimd.tensor_scalar(nbias1[:], nbias1[:], -1.0, 0.0, ALU.mult, ALU.add).then_inc(setup_done, 1)
            nc.gpsimd.tensor_scalar(gb0[:], gb0[:], 0.5, 0.0, ALU.mult, ALU.add).then_inc(setup_done, 1)
            nc.gpsimd.tensor_scalar(gb1[:], gb1[:], 0.5, 0.0, ALU.mult, ALU.add).then_inc(setup_done, 1)
            nc.gpsimd.tensor_scalar(wv0_sb[:], wv0_sb[:], 0.5, 0.0, ALU.mult, ALU.add).then_inc(split_step, 1)
            nc.gpsimd.tensor_scalar(wv1_sb[:], wv1_sb[:], 0.5, 0.0, ALU.mult, ALU.add).then_inc(split_step, 1)
            pool.wait_ge(split_step, 2)
            whole = [(wq0_sb, split0["q"]), (wk0_sb, split0["k"]), (wv0_sb, split0["v"]), (wg0_sb, split0["g"]),
                     (wq1_sb, split1["q"]), (wk1_sb, split1["k"]), (wv1_sb, split1["v"]), (wg1_sb, split1["g"]),
                     (wo1_sb, wo1_parts)]
            for w, parts in whole:
                nc.gpsimd.tensor_scalar(parts[:, 0], w[:], 1.0, 0.0, ALU.mult, ALU.add).then_inc(split_step, 1)
            pool.wait_ge(split_step, 2 + len(whole))
            for w, parts in whole:
                last = nc.gpsimd.tensor_tensor(parts[:, 1], w[:], parts[:, 0], ALU.subtract)
            last.then_inc(setup_done, 1)

            mean, rstd = mean_r[:].rearrange("p r j -> p (r j)"), rstd_r[:].rearrange("p r j -> p (r j)")

            def norm_pair(i, par):
                p = i * 2 + par
                pool.wait_ge(c_loaded[par], i * 48 + 48)
                wait(pool, S0["v"], p * 2 - 2)
                nc.gpsimd.tensor_tensor(xln[:, par], x_in[:, par], mean, ALU.subtract).then_inc(S0["nstep"], 1)
                pool.wait_ge(S0["nstep"], p * 5 + 1)
                nc.gpsimd.tensor_tensor(xln[:, par], xln[:, par], rstd, ALU.mult).then_inc(S0["nstep"], 1)
                pool.wait_ge(S0["nstep"], p * 5 + 2)
                nc.gpsimd.tensor_tensor(xln[:, par], xln[:, par], w_in[:, par], ALU.mult).then_inc(S0["nstep"], 1)
                pool.wait_ge(S0["nstep"], p * 5 + 3)
                nc.gpsimd.tensor_tensor(xln[:, par], xln[:, par], b_in[:, par], ALU.add).then_inc(S0["nstep"], 1)
                pool.wait_ge(S0["nstep"], p * 5 + 4)
                pool.sem_inc(S0["seen"], 1)
                nc.gpsimd.tensor_scalar(xparts[:, par, 0], xln[:, par], 1.0, 0.0, ALU.mult, ALU.add
                                        ).then_inc(S0["nstep"], 1)
                pool.wait_ge(S0["nstep"], p * 5 + 5)
                nc.gpsimd.tensor_tensor(xparts[:, par, 1], xln[:, par], xparts[:, par, 0], ALU.subtract
                                        ).then_inc(S0["ln"], 1)

            def sum_pair(i, par):
                p = i * 2 + par
                wait(pool, S0["fin"], p * 2 + 2)
                wait(pool, S0["sstep"], p * 3)
                nc.gpsimd.tensor_tensor(sqr[:], x1[:, par], x1[:, par], ALU.mult).then_inc(S0["sstep"], 1)
                nc.gpsimd.tensor_tensor(sum1[:, 0], sum1[:, 0], x1[:, par], ALU.add).then_inc(S0["sstep"], 1)
                pool.wait_ge(S0["sstep"], p * 3 + 1)
                nc.gpsimd.tensor_tensor(sum1[:, 1], sum1[:, 1], sqr[:], ALU.add).then_inc(S0["sstep"], 1)

            def residual_pair(i, par):
                p = i * 2 + par
                wait(pool, S0["fin"], p * 2 - 2)
                pool.sem_inc(S0["seen"], 1)
                nc.gpsimd.tensor_scalar(xres[:, par], x_in[:, par], 1.0, rb0[:, 0:1], ALU.mult, ALU.add
                                        ).then_inc(S0["res"], 1)

            pool.wait_ge(stats_ready[0], 1)
            for par in range(2):
                norm_pair(0, par)
                residual_pair(0, par)
            with pool.Fori(1, NP // 2) as i:
                for par in range(2):
                    norm_pair(i, par)
                    sum_pair(i - 1, par)
                    residual_pair(i, par)
            for par in range(2):
                sum_pair(NP // 2 - 1, par)

            mean1 = mean_r[:, 0:1, :].to_broadcast([P, JT, D])
            rstd1 = rstd_r[:, 0:1, :].to_broadcast([P, JT, D])

            def norm_row(i, par):
                r = i * 2 + par
                pool.wait_ge(e_loaded[par], i * 16 + 16)
                wait(pool, S1["xt"], r - 1)
                nc.gpsimd.tensor_tensor(xn[:, par], r_in[:, par], mean1, ALU.subtract).then_inc(S1["nstep"], 1)
                pool.wait_ge(S1["nstep"], r + 1)
                nc.gpsimd.tensor_tensor(xn[:, par], xn[:, par], rstd1, ALU.mult).then_inc(S1["ln"], 1)

            def residual_row(r, par):
                wait(pool, S1["fin"], r - 1)
                nc.gpsimd.tensor_tensor(r_b[:, par], r_in[:, par], bo1_sb[:], ALU.add).then_inc(S1["res"], 1)

            def split_outputs(r):
                wait(pool, S1["gate"], r + 1)
                pool.sem_inc(S1["seen"], 1)
                nc.gpsimd.tensor_scalar(og_parts[:, 0], og_sb[:], 1.0, 0.0, ALU.mult, ALU.add).then_inc(S1["oh"], 1)
                pool.wait_ge(S1["oh"], r + 1)
                nc.gpsimd.tensor_tensor(og_parts[:, 1], og_sb[:], og_parts[:, 0], ALU.subtract).then_inc(S1["oe"], 1)

            pool.wait_ge(stats_ready[1], 1)
            norm_row(0, 0)
            norm_row(0, 1)
            residual_row(0, 0)
            norm_row(1, 0)
            residual_row(1, 1)
            norm_row(1, 1)
            split_outputs(0)
            residual_row(2, 0)
            with pool.Fori(2, NR1 // 2) as i:
                for par in range(2):
                    norm_row(i, par)
                    split_outputs(i * 2 + par - 3)
                    residual_row(i * 2 + par - 1, 1 - par)
            split_outputs(NR1 - 3)
            residual_row(NR1 - 1, 1)
            split_outputs(NR1 - 2)
            split_outputs(NR1 - 1)

        @block.tensor
        def _(pe):
            mm = nc.tensor.matmul
            PARTS = ((0, 0), (0, 1), (1, 0))

            def products(i, k):
                n, par = i * 4 + k, k % 2
                wait(pe, a_out, n - 1)
                pe.wait_ge(a_loaded[k], i * 48 + 48)
                pe.wait_ge(a_prod, n + 1)
                for half in range(CH // BANK):
                    cols = slice(half * BANK, (half + 1) * BANK)
                    for a, src in enumerate((ya[:, par], wa[k], ba[k])):
                        last = mm(psA[par][a * BW:(a + 1) * BW, half, :], wb0_sb[:], src[:, cols],
                                  start=True, stop=True)
                last.then_inc(a_mm, 1)

            pe.wait_ge(wb0_in, 16)
            for k in range(4):
                products(0, k)
            with pe.Fori(1, NCH // 4) as i:
                for k in range(4):
                    products(i, k)

            def totals(k):
                pe.wait_ge(st_red, 2 * k + 2)
                mm(ps[:, 4, 0:2 * GROUPS], ones[:], gsum[:].rearrange("p s g -> p (s g)"),
                   start=True, stop=True).then_inc(st_mm, 1)

            pe.wait_ge(consts_set, CONSTS)
            totals(0)
            pe.wait_ge(weights_in, WEIGHTS)
            pe.wait_ge(setup_done, SETUP_OPS)
            pe.wait_ge(bias_ready, 1)

            def scores0(r, h, par, nth):
                g = r * NH0 + h
                if h == 0:
                    pe.wait_ge(l0_stacked[par], nth * (16 * 4 * HH0))
                wait(pe, S0["exp"], g * 2 - 2)
                m, hh = h // HH0, h % HH0
                for t in range(JT):
                    for a in range(2):
                        last = mm(psS[h % 2][:, t, :], stacked0[:, par, hh, 0, m, t * P:(t + 1) * P],
                                  stacked0[:, par, hh, 1 + a, m, :], start=(a == 0), stop=(a == 1))
                last.then_inc(S0["s"], 1)

            def scores1(r, h, par, nth):
                g = r * NH1 + h
                m, hh = h % MT, h // MT
                if m == 0:
                    pe.wait_ge(l1_stacked[par][hh], nth * (16 * HH1))
                wait(pe, S1["exp"], g * 2 - 2)
                for t in range(JT):
                    last = mm(psS[h % 2][:, t, :], stacked1[:, par, hh, 0, m, t * P:(t + 1) * P],
                              stacked1[:, par, hh, 1, m, :], start=True, stop=True)
                last.then_inc(S1["s"], 1)

            def turn_probs(S, r, h, nh):
                pe.wait_ge(S["exp"], (r * nh + h) * 2 + 2)
                copied(pe, S, r if h >= 2 else r - 1, (h - 2) % nh, nh)
                for t in range(JT):
                    for u in range(JT):
                        last = nc.tensor.transpose(psT[h % 2][:, u, t * P:(t + 1) * P],
                                                   p_sb[:, h % 4, t, u * P:(u + 1) * P], ident_sb[:])
                last.then_inc(S["t"], 1)

            def weigh_values(S, r, half, nh, d, par):
                first, end = half * nh // 2, (half + 1) * nh // 2
                for n in range(first, end):
                    if not any((n in BY_DVE[nh]) == (m in BY_DVE[nh]) for m in range(n + 1, end)):
                        copied(pe, S, r, n, nh)
                if half == 0:
                    pe.wait_ge(S["ve"], r + 1)
                    wait(pe, S["gate"], r)
                for u in range(JT):
                    for h in range(first, end):
                        m, lo = h * d // P, h * d % P
                        last = mm(psO[lo:lo + d, m, :], v_sb[:, par, u, h * d:(h + 1) * d], pT_sb[:, h, u, :],
                                  start=(u == 0), stop=(u == JT - 1), skip_group_check=True)
                last.then_inc(S["av"], 1)

            def turn_sums(S, r, bank):
                pe.wait_ge(S["wide"], r + 1)
                for m in range(MT):
                    for t in range(JT):
                        last = nc.tensor.transpose(psJ[bank][:, m, t * P:(t + 1) * P],
                                                   rwide[:, t, m * P:(m + 1) * P], ident_sb[:])
                last.then_inc(S["r"], 1)

            def row0(b, k, prv, cur, nxt):
                r = b * 4 + k
                k1 = (k + 1) % 4
                xr = [xparts[:, k1 // 2, a, (k1 % 2) * W:(k1 % 2 + 1) * W] for a in range(2)]

                def project(bank, w):
                    for m in range(MT):
                        for n, (a, c) in enumerate(PARTS):
                            last = mm(psJ[bank][:, m, :], w[:, a, m * P:(m + 1) * P], xr[c],
                                      start=(n == 0), stop=(n == 2))
                    return last

                for h in range(NH0):
                    if nxt and h == 0:
                        if k1 % 2 == 0:
                            pe.wait_ge(S0["ln"], (b + (k == 3)) * 2 + k1 // 2 + 1)
                        wait(pe, S0["ge"], r + 1)
                        project(0, split0["q"]).then_inc(S0["q"], 1)
                        wait(pe, S0["ve"], r + 1)
                        project(1, split0["k"]).then_inc(S0["k"], 1)
                    if cur:
                        scores0(r, h, k % 2, b * 2 + k // 2 + 1)
                    if cur and h >= 2:
                        turn_probs(S0, r, h - 2, NH0)
                    if prv and h < 2:
                        turn_probs(S0, r - 1, h + 2, NH0)
                    if prv and h == 1:
                        weigh_values(S0, r - 1, 0, NH0, D0, (k - 1) % 2)
                        wait(pe, S0["fin"], r - 1)
                        turn_sums(S0, r - 1, 2)
                    if prv and h == 2:
                        weigh_values(S0, r - 1, 1, NH0, D0, (k - 1) % 2)
                    if nxt and h == 2:
                        pe.wait_ge(S0["qe"], r + 2)
                        project(0, split0["g"]).then_inc(S0["g"], 1)
                    if nxt and h == 3:
                        pe.wait_ge(S0["ke"], r + 2)
                        for t in range(JT):
                            for n, (a, c) in enumerate(PARTS):
                                last = mm(psJ[1][:, t, :], xr[a][:, t * P:(t + 1) * P], split0["v"][:, c, :],
                                          start=(n == 0), stop=(n == 2))
                        last.then_inc(S0["v"], 1)
                    if prv and h == 3:
                        pe.wait_ge(S0["gate"], r)
                        for m in range(MT):
                            last = mm(psJ[2][:, 0, :], wrep_sb[:, m, :], og_sb[:, m, :],
                                      start=(m == 0), stop=(m == MT - 1))
                        last.then_inc(S0["out"], 1)

            each_row(pe, H, 4, row0)

            totals(1)

            def row1(b, k, prv, cur, nxt):
                r = b * 2 + k
                par = (k + 1) % 2

                def project(bank, w):
                    for m in range(MT):
                        for c in range(MT):
                            for n, (a, e) in enumerate(PARTS):
                                last = mm(psJ[bank][:, m, :], w[:, a, c, m * P:(m + 1) * P], xnT[:, e, c, :],
                                          start=(c + n == 0), stop=(c == MT - 1 and n == 2))
                    return last

                for h in range(NH1):
                    if nxt and h == 0:
                        pe.wait_ge(S1["ln"], r + 2)
                        wait(pe, S1["ge"], r + 1)
                        for m in range(MT):
                            for t in range(JT):
                                last = nc.tensor.transpose(psJ[0][:, m, t * P:(t + 1) * P],
                                                           xn[:, par, t, m * P:(m + 1) * P], ident_sb[:])
                        last.then_inc(S1["xt"], 1)
                    if cur:
                        scores1(r, h, k % 2, b + 1)
                    if cur and h >= 2:
                        turn_probs(S1, r, h - 2, NH1)
                    if prv and h < 2:
                        turn_probs(S1, r - 1, h + 6, NH1)
                    if prv and h == 0:
                        weigh_values(S1, r - 1, 0, NH1, D1, (k - 1) % 2)
                    if nxt and h == 1:
                        pe.wait_ge(S1["xte"], r + 2)
                        wait(pe, S1["ve"], r + 1)
                        project(1, split1["q"]).then_inc(S1["q"], 1)
                    if nxt and h == 2:
                        project(0, split1["k"]).then_inc(S1["k"], 1)
                    if prv and h == 3:
                        wait(pe, S1["fin"], r - 1)
                        turn_sums(S1, r - 1, 2)
                        weigh_values(S1, r - 1, 1, NH1, D1, (k - 1) % 2)
                    if nxt and h == 4:
                        pe.wait_ge(S1["qe"], r + 2)
                        for t in range(JT):
                            for c in range(MT):
                                for n, (a, e) in enumerate(PARTS):
                                    last = mm(psJ[1][:, t, :], xnT[:, a, c, t * P:(t + 1) * P],
                                              split1["v"][:, e, c, :],
                                              start=(c + n == 0), stop=(c == MT - 1 and n == 2))
                        last.then_inc(S1["v"], 1)
                    if nxt and h == 5:
                        pe.wait_ge(S1["ke"], r + 2)
                        project(0, split1["g"]).then_inc(S1["g"], 1)
                    if prv and h >= 6:
                        pe.wait_ge(S1["oe"], r)
                        t = h - 6
                        for m in range(MT):
                            for n, (a, c) in enumerate(PARTS):
                                last = mm(psJ[2][:, t, :], og_parts[:, a, m, t * P:(t + 1) * P],
                                          wo1_parts[:, c, m, :],
                                          start=(m + n == 0), stop=(m == MT - 1 and n == 2))
                        if t == JT - 1:
                            last.then_inc(S1["out"], 1)

            pe.wait_ge(stats_ready[1], 1)
            each_row(pe, NR1, 2, row1)

        @block.scalar
        def _(act):
            def chunk(i, k):
                n, par = i * 4 + k, k % 2
                act.wait_ge(a_loaded[k], i * 48 + 48)
                wait(act, a_sum, n * 2)
                nc.scalar.activation(sq[:, par], xa[k], ACT.Square).then_inc(a_sq, 1)
                act.wait_ge(a_mm, n + 1)
                wait(act, a_stored[par], (i * 2 + k // 2) * 48)
                nc.scalar.activation(prod[:, par].rearrange("p (h n) -> p h n", n=BANK), psA[par],
                                     ACT.Copy).then_inc(a_out, 1)

            for k in range(4):
                chunk(0, k)
            with act.Fori(1, NCH // 4) as i:
                for k in range(4):
                    chunk(i, k)

            def sqrt_of(col, n, count):
                act.wait_ge(st_var, count)
                nc.scalar.activation(st[:, col, 0:n], st[:, col - 1, 0:n], ACT.Sqrt).then_inc(st_sqrt, 1)

            sqrt_of(1, GROUPS, 1)
            sqrt_of(5, 1, 2)
            act.wait_ge(setup_done, SETUP_OPS)

            def exponentials(S, r, h, nh, par):
                act.wait_ge(S["max"], r * nh + h + 1)
                for t in range(JT):
                    nc.scalar.activation(p_sb[:, h % 4, t, :], psS[h % 2][:, t, :], ACT.Exp,
                                         bias=nmax[:, par, 2 * h + t:2 * h + t + 1], scale=-1.0,
                                         accum_out=rsum[:, par, 2 * h + t:2 * h + t + 1]).then_inc(S["exp"], 1)

            def copy_turned(S, g, h):
                act.wait_ge(S["t"], g + 1)
                nc.scalar.activation(pT_sb[:, h], psT[h % 2], ACT.Copy).then_inc(S["pt"], 1)

            def gates(S, r, bank, par, half_bias):
                act.wait_ge(S["g"], r + 1)
                wait(act, S["gr"], r - 1)
                for m in range(MT):
                    last = nc.scalar.activation(th_sb[:, par, m, :], psJ[bank][:, m, :], ACT.Tanh,
                                                bias=half_bias[:, m:m + 1], scale=0.5)
                last.then_inc(S["ge"], 1)

            def row0(b, k, prv, cur, nxt):
                r = b * 4 + k
                par = (k + 1) % 2
                for h in range(NH0):
                    if nxt and h == 0:
                        wait(act, l0_stacked[par], (b * 2 + (k - 1) // 2 + 1) * (16 * 4 * HH0))
                        act.wait_ge(S0["q"], r + 2)
                        nc.scalar.activation(qk_sb[:, par, 0], psJ[0], ACT.Copy, scale=-SCALE0).then_inc(S0["qh"], 1)
                        act.wait_ge(S0["k"], r + 2)
                        nc.scalar.activation(qk_sb[:, par, 2], psJ[1], ACT.Copy).then_inc(S0["kh"], 1)
                    if nxt and h == 3:
                        gates(S0, r + 1, 0, par, gb0)
                    if (cur and h >= 2) or (prv and h < 2):
                        copy_turned(S0, r * NH0 + h - 2, (h - 2) % NH0)
                    if cur:
                        exponentials(S0, r, h, NH0, k % 2)

            each_row(act, H, 4, row0)

            sqrt_of(1, GROUPS, 3)

            def row1(b, k, prv, cur, nxt):
                r = b * 2 + k
                par = (k + 1) % 2
                for h in range(NH1):
                    if nxt and h == 0:
                        act.wait_ge(S1["xt"], r + 2)
                        nc.scalar.activation(xnT[:, 0], psJ[0], ACT.Copy).then_inc(S1["xh"], 1)
                    if nxt and h == 2:
                        for hh in range(HH1):
                            wait(act, l1_stacked[par][hh], (b + k) * (16 * HH1))
                        act.wait_ge(S1["q"], r + 2)
                        nc.scalar.activation(qk_sb[:, par, 0], psJ[1], ACT.Copy, scale=-SCALE1).then_inc(S1["qh"], 1)
                    if nxt and h == 3:
                        act.wait_ge(S1["k"], r + 2)
                        nc.scalar.activation(qk_sb[:, par, 2], psJ[0], ACT.Copy).then_inc(S1["kh"], 1)
                    if (cur and 2 <= h < 6) or (prv and h == 1):
                        copy_turned(S1, r * NH1 + h - 2, (h - 2) % NH1)
                    if nxt and h == 6:
                        gates(S1, r + 1, 0, par, gb1)
                    if cur:
                        exponentials(S1, r, h, NH1, k % 2)

            each_row(act, NR1, 2, row1)

        @block.vector
        def _(dve):
            nc.vector.memset(sum0[:], 0.0).then_inc(a_sum, 2)

            def chunk(i, k):
                n, par = i * 4 + k, k % 2
                dve.wait_ge(a_loaded[k], i * 48 + 48)
                wait(dve, a_mm, n - 1)
                nc.vector.tensor_tensor(ya[:, par], xa[k], wa[k], ALU.mult).then_inc(a_prod, 1)
                dve.wait_ge(a_sum, n * 2 + 2)
                nc.vector.tensor_tensor(sum0[:, 0], sum0[:, 0], xa[k], ALU.add).then_inc(a_sum, 1)
                dve.wait_ge(a_sq, n + 1)
                nc.vector.tensor_tensor(sum0[:, 1], sum0[:, 1], sq[:, par], ALU.add).then_inc(a_sum, 1)

            for k in range(4):
                chunk(0, k)
            with dve.Fori(1, NCH // 4) as i:
                for k in range(4):
                    chunk(i, k)

            done = [0]

            def then(instruction):
                done[0] += 1
                instruction.then_inc(st_step, 1)
                dve.wait_ge(st_step, done[0])

            v = nc.vector
            mean, ex2, var = st[:, 6, :], st[:, 7, :], st[:, 0, :]

            def inverse_root(col, n, to):
                a, root, t = st[:, col, 0:n], st[:, col + 1, 0:n], st[:, col + 2, 0:n]
                then(v.reciprocal(to, root))
                then(v.tensor_tensor(t, to, to, ALU.mult))
                then(v.tensor_tensor(t, t, a, ALU.mult))
                then(v.tensor_scalar(t, t, -0.5, 1.5, ALU.mult, ALU.add))
                then(v.tensor_tensor(to, to, t, ALU.mult))

            def group_stats(sums, rows, k):
                for s in range(2):
                    v.tensor_reduce(gsum[:, s, :], sums[:, s, :].rearrange("p (r g e) -> p g r e", r=rows, e=GS),
                                    AX.XY, ALU.add).then_inc(st_red, 1)
                dve.wait_ge(st_mm, k + 1)
                then(v.tensor_scalar(st[:, 6:8, :], ps[:, 4, 0:2 * GROUPS].rearrange("p (s g) -> p s g", s=2),
                                     1.0 / COUNT, None, ALU.mult))
                then(v.tensor_tensor(st[:, 3, :], mean, mean, ALU.mult))
                then(v.tensor_tensor(st[:, 3, :], ex2, st[:, 3, :], ALU.subtract))
                then(v.tensor_scalar(st[:, 3, :], st[:, 3, :], 0.0, None, ALU.max))

            dve.wait_ge(a_sum, NCH * 2 + 2)
            group_stats(sum0, QR, 0)
            v.tensor_scalar(var, st[:, 3, :], EPS_NORM, None, ALU.add).then_inc(st_var, 1)
            dve.wait_ge(st_var, 1)
            dve.wait_ge(st_sqrt, 1)
            gr = gtot[:, 0, :]
            inverse_root(0, GROUPS, gr)
            then(v.tensor_tensor(st[:, 2, :], gr, gr, ALU.mult))
            then(v.tensor_tensor(st[:, 2, :], st[:, 2, :], st[:, 3, :], ALU.mult))
            then(v.tensor_reduce(tall[:, 0:1], st[:, 2, :], AX.X, ALU.add))
            v.tensor_scalar(st[:, 4, 0:1], tall[:, 0:1], 1.0 / GROUPS, EPS_NORM, ALU.mult, ALU.add
                            ).then_inc(st_var, 1)
            dve.wait_ge(st_var, 2)
            dve.wait_ge(st_sqrt, 2)
            inverse_root_1 = tall[:, 1:2]
            then(v.reciprocal(inverse_root_1, st[:, 5, 0:1]))
            then(v.tensor_tensor(tall[:, 2:3], inverse_root_1, inverse_root_1, ALU.mult))
            then(v.tensor_tensor(tall[:, 2:3], tall[:, 2:3], st[:, 4, 0:1], ALU.mult))
            then(v.tensor_scalar(tall[:, 2:3], tall[:, 2:3], -0.5, 1.5, ALU.mult, ALU.add))
            then(v.tensor_tensor(inverse_root_1, inverse_root_1, tall[:, 2:3], ALU.mult))
            then(v.tensor_scalar(gr, gr, inverse_root_1, None, ALU.mult))

            def spread(r):
                for dst, src in ((mean_r, mean), (rstd_r, gr)):
                    then(v.tensor_copy(dst[:, r, :].rearrange("p (g e) -> p g e", e=GS),
                                       src.unsqueeze(2).to_broadcast([P, GROUPS, GS])))

            for r in range(PR):
                spread(r)
            dve.wait_ge(parts_in, 16 * 3 * JT)
            parts = [parts_sb[:, a].rearrange("p h t k -> p (h t) k") for a in range(3)]
            wide = [P, NH0 * JT, W]
            then(v.tensor_tensor(parts[1], parts[1], mean_r[:, 0:1, :].to_broadcast(wide), ALU.mult))
            then(v.tensor_tensor(parts[0], parts[0], parts[1], ALU.subtract))
            then(v.tensor_tensor(parts[0], parts[0], rstd_r[:, 0:1, :].to_broadcast(wide), ALU.mult))
            flat = [parts_sb[:, a].rearrange("p h t k -> p (h t k)") for a in (0, 2)]
            v.scalar_tensor_tensor(out=nbias0[:].rearrange("p h t k -> p (h t k)"), in0=flat[0], scalar=-1.0,
                                   in1=flat[1], op0=ALU.mult, op1=ALU.subtract).then_inc(bias_ready, 1)
            dve.wait_ge(bias_ready, 1)
            v.tensor_copy(tall[:, 3:4], tall[:, 1:2]).then_inc(stats_ready[0], 1)
            dve.wait_ge(setup_done, SETUP_OPS)
            dve.wait_ge(consts_set, CONSTS)

            def bias_and_max(S, r, h, nh, par, nbias):
                dve.wait_ge(S["s"], r * nh + h + 1)
                dve.sem_inc(S["seen"], 1)
                for t in range(JT):
                    last = v.tensor_tensor_reduce(psS[h % 2][:, t, :], psS[h % 2][:, t, :], nbias[:, h, t, :], 1.0, BIG,
                                           ALU.add, ALU.min, nmax[:, par, 2 * h + t:2 * h + t + 1])
                last.then_inc(S["max"], 1)

            def invert_sums(S, r, nh, par):
                dve.wait_ge(S["exp"], (r + 1) * nh * 2)
                v.reciprocal(rinv[:, 0:nh * JT], rsum[:, par, 0:nh * JT]).then_inc(S["den"], 1)
                dve.wait_ge(S["den"], r + 1)
                v.tensor_copy(rwide[:].rearrange("p t (h e) -> p t h e", h=nh),
                              rinv[:, 0:nh * JT].rearrange("p (h t) -> p t h", t=JT).unsqueeze(3)
                              .to_broadcast([P, JT, nh, MT * P // nh])).then_inc(S["wide"], 1)

            def gates_over_sums(S, r, bank, par):
                dve.wait_ge(S["r"], r + 1)
                dve.wait_ge(S["ge"], r + 1)
                v.scalar_tensor_tensor(out=gr_sb[:].rearrange("p m j -> p (m j)"),
                                       in0=th_sb[:, par].rearrange("p m j -> p (m j)"), scalar=1.0,
                                       in1=psJ[bank].rearrange("p m j -> p (m j)"),
                                       op0=ALU.add, op1=ALU.mult).then_inc(S["gr"], 1)

            def gate_outputs(S, r):
                dve.wait_ge(S["av"], (r + 1) * 2)
                dve.wait_ge(S["gr"], r + 1)
                v.tensor_tensor(og_sb[:], psO, gr_sb[:], ALU.mult).then_inc(S["gate"], 1)

            def copy_values(S, r, bank, par):
                dve.wait_ge(S["v"], r + 1)
                v.tensor_copy(v_sb[:, par], psJ[bank]).then_inc(S["ve"], 1)

            def low_part(dst, high, src, scale, done, sem_low, count):
                dve.wait_ge(done, count)
                v.scalar_tensor_tensor(out=dst.rearrange("p m j -> p (m j)"), in0=src.rearrange("p m j -> p (m j)"),
                                       scalar=scale, in1=high.rearrange("p m j -> p (m j)"),
                                       op0=ALU.mult, op1=ALU.subtract).then_inc(sem_low, 1)

            def row0(b, k, prv, cur, nxt):
                r = b * 4 + k
                par = (k + 1) % 2
                for h in range(NH0):
                    if nxt and h == 0:
                        low_part(qk_sb[:, par, 1], qk_sb[:, par, 0], psJ[0], -SCALE0, S0["qh"], S0["qe"], r + 2)
                    if prv and h == 3:
                        gate_outputs(S0, r - 1)
                    if cur:
                        bias_and_max(S0, r, h, NH0, k % 2, nbias0)
                    if prv and h == 0:
                        invert_sums(S0, r - 1, NH0, par)
                    if nxt and h == 0:
                        low_part(qk_sb[:, par, 3], qk_sb[:, par, 2], psJ[1], 1.0, S0["kh"], S0["ke"], r + 2)
                    if prv and h == 2:
                        gates_over_sums(S0, r - 1, 2, par)
                    if nxt and h == 3:
                        copy_values(S0, r + 1, 1, par)
                    if prv and h == 3:
                        kp = (k - 1) % 4
                        pair, half = kp // 2, kp % 2
                        dve.wait_ge(S0["out"], r)
                        if half == 0:
                            i = b - (k == 0)
                            dve.wait_ge(S0["res"], i * 2 + pair + 1)
                            wait(dve, S0["sstep"], (i * 2 + pair - 1) * 3)
                            wait(dve, c_stored[pair], i * 16)
                        v.tensor_tensor(x1[:, pair, half * W:(half + 1) * W], psJ[2][:, 0, :],
                                        xres[:, pair, half * W:(half + 1) * W], ALU.add).then_inc(S0["fin"], 1)

            each_row(dve, H, 4, row0)

            dve.wait_ge(S0["sstep"], NP * 3)
            group_stats(sum1, PR, 1)
            v.tensor_scalar(var, st[:, 3, :], EPS_NORM, None, ALU.add).then_inc(st_var, 1)
            dve.wait_ge(st_var, 3)
            dve.wait_ge(st_sqrt, 3)
            inverse_root(0, GROUPS, gr)
            spread(0)
            v.tensor_copy(tall[:, 3:4], gr[:, 0:1]).then_inc(stats_ready[1], 1)

            def row1(b, k, prv, cur, nxt):
                r = b * 2 + k
                par = (k + 1) % 2
                for h in range(NH1):
                    if prv and h == 4:
                        gate_outputs(S1, r - 1)
                    if cur:
                        bias_and_max(S1, r, h, NH1, k % 2, nbias1)
                    if nxt and h == 0:
                        low_part(xnT[:, 1], xnT[:, 0], psJ[0], 1.0, S1["xh"], S1["xte"], r + 2)
                    if (cur and h >= 6) or (prv and h == 0):
                        dve.wait_ge(S1["t"], r * NH1 + h - 1)
                        v.tensor_copy(pT_sb[:, (h - 2) % NH1], psT[h % 2]).then_inc(S1["ptv"], 1)
                    if prv and h == 1:
                        invert_sums(S1, r - 1, NH1, par)
                    if nxt and h == 2:
                        low_part(qk_sb[:, par, 1], qk_sb[:, par, 0], psJ[1], -SCALE1, S1["qh"], S1["qe"], r + 2)
                    if nxt and h == 3:
                        low_part(qk_sb[:, par, 3], qk_sb[:, par, 2], psJ[0], 1.0, S1["kh"], S1["ke"], r + 2)
                    if prv and h == 3:
                        gates_over_sums(S1, r - 1, 2, par)
                    if nxt and h == 5:
                        copy_values(S1, r + 1, 1, par)
                    if prv and h == 7:
                        dve.wait_ge(S1["out"], r)
                        dve.wait_ge(S1["res"], r)
                        wait(dve, e_stored[par], (b - (k == 0)) * 16)
                        v.tensor_tensor(y_sb[:, par], psJ[2], r_b[:, par], ALU.add).then_inc(S1["fin"], 1)

            each_row(dve, NR1, 2, row1)


def kernel(**inputs):
    import numpy as _np
    import concourse.bacc as _bacc
    from concourse import mybir as _mybir
    from concourse.bass_utils import run_bass_kernel_spmd as _run

    def a(name):
        return _np.asarray(inputs[name])

    def pairs_first(w):
        return w.reshape(w.shape[0], 4, 2, 32).transpose(0, 2, 1, 3).reshape(w.shape)

    C, H, W = a("x").shape[1:]
    nh0 = a("L0_conv_wb").shape[0]
    hc0 = a("L0_conv_wq").shape[0]
    given = {
        "x": a("x")[0], "ln_w": a("L0_conv_ln_w"), "ln_b": a("L0_conv_ln_b"),
        "wq0": a("L0_conv_wq").T, "wk0": a("L0_conv_wk").T, "wv0": a("L0_conv_wv").T, "wg0": a("L0_conv_wg_w").T,
        "wb0": a("L0_conv_wb").T, "wg0_b": a("L0_conv_wg_b").reshape(-1, 128).T,
        "wrep": a("L0_conv_wrep_w").reshape(C, hc0 // nh0, nh0).transpose(2, 1, 0).reshape(hc0, C),
        "wrep_b": a("L0_conv_wrep_b").reshape(C, 1),
        "pair_bias1": a("L1_conv_nonbatched_bias")[0],
        "wq1": pairs_first(a("L1_conv_Wq").T), "wk1": pairs_first(a("L1_conv_Wk").T), "wv1": a("L1_conv_Wv").T, "wg1": a("L1_conv_Wg").T,
        "wg1_b": a("L1_conv_gating_bias").reshape(-1, 128).T,
        "wo1": a("L1_conv_Wo").T, "bo1": a("L1_conv_bo"),
        "ident": _np.eye(128, dtype=_np.float32),
    }
    nc = _bacc.Bacc("TRN2", target_bir_lowering=False, num_devices=1)
    arrays, args = {}, []
    for name, array in given.items():
        array = _np.ascontiguousarray(array)
        arrays[f"in_{name}_dram"] = array
        args.append(nc.dram_tensor(f"in_{name}_dram", array.shape, _mybir.dt.from_np(array.dtype),
                                   kind="ExternalInput").ap())
    args.append(nc.dram_tensor("out_0_dram", (C, H, W), _mybir.dt.float32, kind="ExternalOutput").ap())
    two_layers(nc, *args)
    r = _run(nc, [arrays], core_ids=[0])
    return r.results[0]["out_0_dram"].reshape(1, C, H, W)
```
